# Optimizing a Trainium2 kernel written in Bass

```python
import numpy as np
import jax
import jax.numpy as jnp

def _softmax(x, axis=-1):
    return jax.nn.softmax(x, axis=axis)

def _gelu(x):
    return jax.nn.gelu(x, approximate=True)

def _silu(x):
    return jax.nn.silu(x)

def _sigmoid(x):
    return jax.nn.sigmoid(x)

def _layernorm(x, axis=-1, eps=1e-05):
    m = jnp.mean(x, axis=axis, keepdims=True)
    v = jnp.var(x, axis=axis, keepdims=True)
    return (x - m) / jnp.sqrt(v + eps)

def _scatter_add(tgt, idx, src, axis=0):
    return tgt.at[idx].add(src)

def _segment_sum(src, seg, n):
    return jax.ops.segment_sum(src, seg, n)
kernel_name = 'mk_gnn_resnorm_d4_gnn_r8_fa325d'

def setup_inputs(seed: int=0):
    np.random.seed(seed)
    _w = jnp.asarray

    def _rec_inputs():
        import jax
        import jax.numpy as jnp
        _gk = jax.random.key(seed)
        x = -0.0001006 + 1 * jax.random.normal(jax.random.fold_in(_gk, 1), (12500, 48), jnp.float32)
        src = jax.random.randint(jax.random.fold_in(_gk, 2), (200000,), 0, 12500, jnp.int32)
        dst = jax.random.randint(jax.random.fold_in(_gk, 3), (200000,), 0, 12500, jnp.int32)
        _o = jnp.argsort(dst, stable=True)
        src = src[_o]
        dst = dst[_o]
        edge_attr_40 = jax.random.uniform(jax.random.fold_in(_gk, 13), (200000, 40), jnp.float32, 0.0, 1)
        edge_weight = jax.random.uniform(jax.random.fold_in(_gk, 15), (200000,), jnp.float32, 0.0, 6.99999)
        edge_weight1 = -0.000414295 + 0.999828 * jax.random.normal(jax.random.fold_in(_gk, 16), (200000, 1), jnp.float32)
        node_type_119 = jax.random.randint(jax.random.fold_in(_gk, 17), (12500,), 0, 119, jnp.int32)
        node_vec = jax.random.uniform(jax.random.fold_in(_gk, 18), (12500,), jnp.float32, 0.0, 1.49999)
        return (x, src, dst, edge_attr_40, edge_weight, edge_weight1, node_type_119, node_vec)
    x, src, dst, edge_attr_40, edge_weight, edge_weight1, node_type_119, node_vec = _rec_inputs()

    def _L0_gnn_setup():
        import jax, jax.numpy as jnp
        import numpy as np
        N_NODES = 12500
        N_EDGES = 200000
        N_CLASSES = 48
        key = jax.random.key(seed)
        k1, k2, k3, k4 = jax.random.split(key, 4)
        soft_label = jax.random.normal(k1, (N_NODES, N_CLASSES), dtype=jnp.float32)
        e = jax.random.normal(k2, (N_EDGES, 1), dtype=jnp.float32)
        src = jax.random.randint(k3, (N_EDGES,), 0, N_NODES)
        dst = jax.random.randint(k4, (N_EDGES,), 0, N_NODES)
        return {'soft_label': soft_label, 'e': e, 'src': src, 'dst': dst}
    _L0_gnn_all = _L0_gnn_setup()
    _L0_gnn_in = {k: v for k, v in _L0_gnn_all.items() if k in ()}
    del _L0_gnn_all

    def _L1_gnn_setup():
        import jax, jax.numpy as jnp
        import numpy as np
        CUTOFF = 6.0
        LN_EPS = 1e-05
        key = jax.random.key(seed)
        ks = jax.random.split(key, 16)
        N, E, H, R, NEL, G = (6250, 100000, 48, 40, 119, 32)
        inp = {'h': jax.random.normal(ks[0], (N, H), jnp.float32), 'edge_index': jax.random.randint(ks[1], (2, E), 0, N, jnp.int64), 'edge_attr': jax.random.uniform(ks[2], (E, R), jnp.float32), 'distances': jax.random.uniform(ks[3], (E,), jnp.float32) * 7.0, 'atom_z': jax.random.randint(ks[4], (N,), 0, NEL, jnp.int64), 'node_mult': jax.random.uniform(ks[5], (N,), jnp.float32) + 0.5, 'batch': jnp.zeros((N,), jnp.int64), 'W1': jax.random.normal(ks[6], (H, R), jnp.float32) / np.sqrt(R), 'b1': jax.random.normal(ks[7], (H,), jnp.float32) * 0.01, 'W2': jax.random.normal(ks[8], (H, H), jnp.float32) / np.sqrt(H), 'b2': jax.random.normal(ks[9], (H,), jnp.float32) * 0.01, 'emb': jax.random.normal(ks[10], (NEL, G), jnp.float32) * 0.01, 'adaptW': jax.random.normal(ks[11], (G, G), jnp.float32) * 0.01, 'gamma': jnp.ones((H,), jnp.float32), 'beta': jnp.zeros((H,), jnp.float32)}
        return inp
    _L1_gnn_all = _L1_gnn_setup()
    _L1_gnn_in = {k: v for k, v in _L1_gnn_all.items() if k in ('W1', 'b1', 'W2', 'b2', 'emb', 'adaptW', 'gamma', 'beta')}
    del _L1_gnn_all

    def _L2_gnn_setup():
        import jax, jax.numpy as jnp
        import numpy as np
        N_NODES = 12500
        N_EDGES = 200000
        D_IN = 48
        D_H = 48
        D_OUT = 48

        def _graph_conv(x, src, dst, w_rel, w_root, b, num_nodes):
            agg = jax.ops.segment_sum(x[src], dst, num_segments=num_nodes)
            return agg @ w_rel + x @ w_root + b
        key = jax.random.key(seed)
        ks = jax.random.split(key, 8)
        s = 0.05
        x = jax.random.normal(ks[0], (N_NODES, D_IN), dtype=jnp.float32)
        edge_index = jax.random.randint(ks[1], (2, N_EDGES), 0, N_NODES, dtype=jnp.int64)
        w_rel1 = jax.random.normal(ks[2], (D_IN, D_H), dtype=jnp.float32) * s
        w_root1 = jax.random.normal(ks[3], (D_IN, D_H), dtype=jnp.float32) * s
        b1 = jax.random.normal(ks[4], (D_H,), dtype=jnp.float32) * s
        w_rel2 = jax.random.normal(ks[5], (D_H, D_OUT), dtype=jnp.float32) * s
        w_root2 = jax.random.normal(ks[6], (D_H, D_OUT), dtype=jnp.float32) * s
        b2 = jax.random.normal(ks[7], (D_OUT,), dtype=jnp.float32) * s
        return {'x': x, 'edge_index': edge_index, 'w_rel1': w_rel1, 'w_root1': w_root1, 'b1': b1, 'w_rel2': w_rel2, 'w_root2': w_root2, 'b2': b2}
    _L2_gnn_all = _L2_gnn_setup()
    _L2_gnn_in = {k: v for k, v in _L2_gnn_all.items() if k in ('w_rel1', 'w_root1', 'b1', 'w_rel2', 'w_root2', 'b2')}
    del _L2_gnn_all

    def _L3_gnn_setup():
        import jax, jax.numpy as jnp
        import numpy as np
        N_NODES = 6250
        N_EDGES = 200000
        D_IN = 48
        D_OUT = 48
        K = 4
        key = jax.random.key(seed)
        k1, k2, k3, k4, k5 = jax.random.split(key, 5)
        x = jax.random.normal(k1, (N_NODES, D_IN), dtype=jnp.float32)
        edge_index = jax.random.randint(k2, (2, N_EDGES), 0, N_NODES, dtype=jnp.int64)
        weight = jax.random.normal(k3, (K, D_IN, D_OUT), dtype=jnp.float32) * (1.0 / np.sqrt(D_IN))
        bias = jax.random.normal(k4, (D_OUT,), dtype=jnp.float32) * 0.01
        return {'x': x, 'edge_index': edge_index, 'weight': weight, 'bias': bias}
    _L3_gnn_all = _L3_gnn_setup()
    _L3_gnn_in = {k: v for k, v in _L3_gnn_all.items() if k in ('weight', 'bias')}
    del _L3_gnn_all
    return {'x': x, 'src': src, 'dst': dst, 'edge_attr_40': edge_attr_40, 'edge_weight': edge_weight, 'edge_weight1': edge_weight1, 'node_type_119': node_type_119, 'node_vec': node_vec, 'L1_gnn_W1': _L1_gnn_in['W1'], 'L1_gnn_b1': _L1_gnn_in['b1'], 'L1_gnn_W2': _L1_gnn_in['W2'], 'L1_gnn_b2': _L1_gnn_in['b2'], 'L1_gnn_emb': _L1_gnn_in['emb'], 'L1_gnn_adaptW': _L1_gnn_in['adaptW'], 'L1_gnn_gamma': _L1_gnn_in['gamma'], 'L1_gnn_beta': _L1_gnn_in['beta'], 'L2_gnn_w_rel1': _L2_gnn_in['w_rel1'], 'L2_gnn_w_root1': _L2_gnn_in['w_root1'], 'L2_gnn_b1': _L2_gnn_in['b1'], 'L2_gnn_w_rel2': _L2_gnn_in['w_rel2'], 'L2_gnn_w_root2': _L2_gnn_in['w_root2'], 'L2_gnn_b2': _L2_gnn_in['b2'], 'L3_gnn_weight': _L3_gnn_in['weight'], 'L3_gnn_bias': _L3_gnn_in['bias']}

def reference(x, src, dst, edge_attr_40, edge_weight, edge_weight1, node_type_119, node_vec, L1_gnn_W1, L1_gnn_b1, L1_gnn_W2, L1_gnn_b2, L1_gnn_emb, L1_gnn_adaptW, L1_gnn_gamma, L1_gnn_beta, L2_gnn_w_rel1, L2_gnn_w_root1, L2_gnn_b1, L2_gnn_w_rel2, L2_gnn_w_root2, L2_gnn_b2, L3_gnn_weight, L3_gnn_bias):
    import jax
    import jax.numpy as jnp

    def _L0_gnn_ref(soft_label, e, src, dst):
        import jax, jax.numpy as jnp
        import numpy as np
        N_NODES = 12500
        N_EDGES = 200000
        N_CLASSES = 48
        N = soft_label.shape[0]
        logits = e[:, 0]
        seg_max = jax.ops.segment_max(logits, dst, num_segments=N)
        seg_max = jnp.where(jnp.isfinite(seg_max), seg_max, 0.0)
        ex = jnp.exp(logits - seg_max[dst])
        seg_sum = jax.ops.segment_sum(ex, dst, num_segments=N)
        a = ex / seg_sum[dst]
        msg = soft_label[src] * a[:, None]
        rst = jax.ops.segment_sum(msg, dst, num_segments=N)
        return jax.nn.elu(rst)

    def _L1_gnn_ref(h, edge_index, edge_attr, distances, atom_z, node_mult, batch, W1, b1, W2, b2, emb, adaptW, gamma, beta):
        import jax, jax.numpy as jnp
        import numpy as np
        CUTOFF = 6.0
        LN_EPS = 1e-05
        src, dst = (edge_index[0], edge_index[1])
        N = h.shape[0]
        gate = jax.nn.silu(edge_attr @ W1.T + b1) @ W2.T + b2
        ei = emb[atom_z[src]]
        ej = emb[atom_z[dst]]
        adapt_logit = jnp.sum(ei * (ej @ adaptW.T), axis=-1, keepdims=True)
        gate = gate + adapt_logit
        cw = jnp.where(distances < CUTOFF, 0.5 * (jnp.cos(jnp.pi * distances / CUTOFF) + 1.0), 0.0)
        mj = node_mult[dst]
        msg = gate * h[dst] * (cw * mj)[:, None]
        agg = jax.ops.segment_sum(msg, src, num_segments=N)
        tot = jax.ops.segment_sum(mj, src, num_segments=N)
        agg = agg / jnp.clip(tot, 1e-08, None)[:, None]
        x = h + agg
        mu = jnp.mean(x, axis=-1, keepdims=True)
        var = jnp.mean(jnp.square(x - mu), axis=-1, keepdims=True)
        return (x - mu) / jnp.sqrt(var + LN_EPS) * gamma + beta

    def _L2_gnn_ref(x, edge_index, w_rel1, w_root1, b1, w_rel2, w_root2, b2):
        import jax, jax.numpy as jnp
        import numpy as np
        N_NODES = 12500
        N_EDGES = 200000
        D_IN = 48
        D_H = 48
        D_OUT = 48

        def _graph_conv(x, src, dst, w_rel, w_root, b, num_nodes):
            agg = jax.ops.segment_sum(x[src], dst, num_segments=num_nodes)
            return agg @ w_rel + x @ w_root + b
        src, dst = (edge_index[0], edge_index[1])
        n = x.shape[0]
        h = jax.nn.relu(_graph_conv(x, src, dst, w_rel1, w_root1, b1, n))
        out = _graph_conv(h, src, dst, w_rel2, w_root2, b2, n)
        return out

    def _L3_gnn_ref(x, edge_index, weight, bias):
        import jax, jax.numpy as jnp
        import numpy as np
        N_NODES = 6250
        N_EDGES = 200000
        D_IN = 48
        D_OUT = 48
        K = 4
        'PyG ChebConv forward with sym normalization, lambda_max=2.0.\n\n            L_hat = 2L/lambda_max - I. With lambda_max=2 and sym Laplacian, the\n            diagonal becomes 0 and off-diagonal weights are -d_i^{-1/2} d_j^{-1/2}.\n            T0 = x, T1 = L_hat x, Tk = 2 L_hat T_{k-1} - T_{k-2};  out = sum_k Tk W_k + b.\n            '
        n = x.shape[0]
        row, col = (edge_index[0], edge_index[1])
        ew = (row != col).astype(x.dtype)
        deg = jax.ops.segment_sum(ew, row, num_segments=n)
        dis = jnp.where(deg > 0, jax.lax.rsqrt(deg), 0.0)
        w = -dis[row] * ew * dis[col]

        def prop(h):
            return jax.ops.segment_sum(w[:, None] * h[row], col, num_segments=n)
        tx0 = x
        out = tx0 @ weight[0]
        tx1 = prop(x)
        out = out + tx1 @ weight[1]
        for k in range(2, weight.shape[0]):
            tx2 = 2.0 * prop(tx1) - tx0
            out = out + tx2 @ weight[k]
            tx0, tx1 = (tx1, tx2)
        return out + bias
    edge_index = jnp.stack([src, dst])
    batch0 = jnp.zeros((12500,), jnp.int32)
    x = _layernorm(x + _L0_gnn_ref(x, edge_weight1, src, dst), axis=-1)
    x = _layernorm(x + _L1_gnn_ref(x, edge_index, edge_attr_40, edge_weight, node_type_119, node_vec, batch0, L1_gnn_W1, L1_gnn_b1, L1_gnn_W2, L1_gnn_b2, L1_gnn_emb, L1_gnn_adaptW, L1_gnn_gamma, L1_gnn_beta), axis=-1)
    x = _layernorm(x + _L2_gnn_ref(x, edge_index, L2_gnn_w_rel1, L2_gnn_w_root1, L2_gnn_b1, L2_gnn_w_rel2, L2_gnn_w_root2, L2_gnn_b2), axis=-1)
    x = _layernorm(x + _L3_gnn_ref(x, edge_index, L3_gnn_weight, L3_gnn_bias), axis=-1)
    return x

_drawn_inputs = setup_inputs


def setup_inputs(seed=0):
    import zlib

    import numpy as np

    out = dict(_drawn_inputs(seed))
    spreads = {'L1_gnn_gamma': (1.0, 0.2), 'L1_gnn_beta': (0.0, 0.1)}
    factors = {'edge_attr_40': 7.64,
     'edge_weight': 6.472,
     'node_vec': 7.731,
     'L1_gnn_W1': 4.024,
     'L1_gnn_b1': 200.0,
     'L1_gnn_W2': 3.567,
     'L1_gnn_b2': 200.0,
     'L1_gnn_emb': 64.0,
     'L1_gnn_adaptW': 64.0,
     'L2_gnn_b2': 2.872,
     'L3_gnn_bias': 8.0}
    for name, (base, spread) in spreads.items():
        noise = np.random.default_rng([zlib.crc32(name.encode()), seed]).standard_normal(out[name].shape)
        drawn = base * np.exp(spread * noise) if base else spread * noise
        out[name] = jnp.asarray(drawn.astype(out[name].dtype))
    for name, factor in factors.items():
        out[name] = (out[name] * factor).astype(out[name].dtype)
    return out
```

```python
import concourse.bass as bass
from concourse import mybir
from contextlib import ExitStack

F32 = mybir.dt.float32
I32 = mybir.dt.int32
ALU = mybir.AluOpType
ACT = mybir.ActivationFunctionType
AX = mybir.AxisListType

N = 12500
E = 200000
D = 48
R = 40
TYPES = 119
GE = 32
P = 128
NB = -(-N // P)
NP = NB * P
UG = 4
UI = 4
STEPS = -(-E // (P * UG * UI))
GROUPS = STEPS * UI
CHUNKS = GROUPS * UG
KT = -(-CHUNKS // P)
ROWS = KT * P
FULL = E // P
REST = E - FULL * P
PAD_DST = 20000
BIG = 1.5e38
ACC_W = NP + P
EPS = 1e-5
IDX_SPARE = 2 * NP
SCAT_ROWS = NP + P
RB = 7
RSTEPS = NB // (2 * RB)


def run_steps(engine, body):
    body(0, True, False)
    with engine.Fori(1, STEPS - 1) as it:
        body(it, False, False)
    body(STEPS - 1, False, True)


def gnn(nc, a, out):
    ROLES.clear()
    ctx = ExitStack()
    with ctx:
        def dram(name, shape, dt=F32):
            return nc.dram_tensor(name, shape, dt).ap()

        def sb(name, shape, dt=F32, c=ctx):
            return c.enter_context(nc.sbuf_tensor(name, shape, dt))

        tab_in = dram("tab_in", (NP, D + GE))
        tab_dst = dram("tab_dst", (NP, D + 1 + GE))
        tab_type = dram("tab_type", (TYPES, 2 * GE))
        tab_h = [dram(f"tab_h{i}", (NP, D)) for i in range(5)]
        emb_edge = dram("emb_edge", (CHUNKS * P, GE))
        rank50 = dram("rank50", (IDX_SPARE, D + 2))
        rank48 = [dram(f"rank48{i}", (IDX_SPARE, D)) for i in range(3)]
        rank96 = dram("rank96", (IDX_SPARE, 2 * D))
        rank144 = dram("rank144", (IDX_SPARE, 3 * D))
        scat = [dram(f"scat{i}", (SCAT_ROWS, D + 2)) for i in range(UG)]

        ident = sb("ident", [P, P])
        iota_row = sb("iota_row", [P, P])
        tril = sb("tril", [P, P])
        ones_row = sb("ones_row", [1, P])
        spare_id = sb("spare_id", [P, 1])
        src_i = sb("src_i", [P, CHUNKS], I32)
        dst_i = sb("dst_i", [P, CHUNKS], I32)
        src_f = sb("src_f", [P, CHUNKS])
        loc = sb("loc", [P, CHUNKS + UG])
        loc_ns = sb("loc_ns", [P, CHUNKS + UG])
        exs = sb("exs", [P, CHUNKS + UG, 2])
        cut = sb("cut", [P, CHUNKS])
        win_row = sb("win_row", [1, ROWS], I32)
        node_idx = sb("node_idx", [P, NB], I32)
        dis = sb("dis", [P, NB])
        mult = sb("mult", [P, NB])
        stat = [sb(f"stat{i}", [P, NB]) for i in range(2)]
        X = sb("X", [P, NB, D])
        w1T = sb("w1T", [R, D])
        b1c = sb("b1c", [D, 1])
        w2T = sb("w2T", [D, D])
        b2r = sb("b2r", [1, D])
        gam = sb("gam", [P, D])
        bet = sb("bet", [P, D])
        eps_c = sb("eps_c", [P, 1])
        wrel1 = sb("wrel1", [D, D])
        wrel2 = sb("wrel2", [D, D])
        wroot1 = sb("wroot1", [D, D])
        wroot2 = sb("wroot2", [D, D])
        l2b1 = sb("l2b1", [1, D])
        l2b2 = sb("l2b2", [1, D])
        l3b = sb("l3b", [1, D])
        w3i13 = sb("w3i13", [D, 3 * D])
        w3i2 = sb("w3i2", [D, 2 * D])
        w302 = sb("w302", [D, D])
        id50 = sb("id50", [D + 2, D + 2])

        setup(nc, a, dict(locals()))

        arena = sb("arena", [P, ACC_W])
        OUT = sb("OUT", [P, NB, D])
        TMP = sb("TMP", [P, NB, D])
        L = dict(locals())
        gather_pass(nc, L, "p0", tab_in, D + GE, loc, weights=True, emb_edge=emb_edge)
        rank_nodes(nc, L)
        rank_rows(nc, L, "r0", id50, D + 2, D + 2, rank50)
        nodes0(nc, L)
        edge_pass(nc, L, a)
        nodes1(nc, L)
        gather_pass(nc, L, "p2", tab_h[0], D, loc, dense=(wroot1, l2b1))
        rank_rows(nc, L, "r2", wrel1, D, D, rank48[0])
        nodes2a(nc, L)
        gather_pass(nc, L, "p3", tab_h[1], D, loc, dense=(wroot2, l2b2), dense_in="TMP")
        rank_rows(nc, L, "r3", wrel2, D, D, rank48[1])
        nodes2b(nc, L)
        gather_pass(nc, L, "p4", tab_h[2], D, loc_ns, dense=(w302, l3b))
        rank_rows(nc, L, "r4", w3i13, D, 3 * D, rank144)
        nodes3a(nc, L)
        gather_pass(nc, L, "p5", tab_h[3], D, loc_ns)
        rank_rows(nc, L, "r5", w3i2, D, 2 * D, rank96)
        nodes3b(nc, L)
        gather_pass(nc, L, "p6", tab_h[4], D, loc_ns)
        rank_rows(nc, L, "r6", w3i13[:, 2 * D:3 * D], D, D, rank48[2])
        nodes3c(nc, L, out)


def node_rows(table, lo, hi, width):
    return table[0:NP, :].rearrange("(p b) d -> p b d", b=NB)[:, :, lo:hi]


ZW = NB * D // 4
LAST_P = N // NB
LAST_B = N - LAST_P * NB


def setup(nc, a, L):
    def g(n):
        return L[n]
    ident, X, mult = g("ident"), g("X"), g("mult")
    with ExitStack() as c:
        def sb(name, shape, dt=F32):
            return c.enter_context(nc.sbuf_tensor(name, shape, dt))

        def sem(name):
            return c.enter_context(nc.semaphore(name))
        FW = KT * P
        s_i = sb("s_i", [P, KT, P], I32)
        d_i = sb("d_i", [P, KT, P], I32)
        pl_i = sb("pl_i", [P, KT], I32)
        nf_i = sb("nf_i", [P, KT], I32)
        S = sb("S", [P, KT, P])
        Dd = sb("Dd", [P, KT, P])
        pl = sb("pl", [P, KT])
        nf = sb("nf", [P, KT])
        LG = sb("LG", [P, KT, P])
        DIST = sb("DIST", [P, KT, P])
        V = sb("V", [P, KT, P])
        F = sb("F", [P, KT, P])
        Q = sb("Q", [P, KT, P])
        Mx = s_i[:].bitcast(F32)
        T1 = d_i[:].bitcast(F32)
        PR = sb("PR", [P, KT, P])
        halfpi = sb("halfpi", [P, 1])
        col = [sb(f"col{i}", [P, KT]) for i in range(6)]
        car = sb("car", [P, KT])
        rows = [t[0:1, :, :].rearrange("o k q -> o (k q)") for t in (PR, S, V, DIST)]
        z_i = sb("z_i", [P, NB], I32)
        EP = sb("EP", [P, NB, 2 * GE])
        zero = sb("zero", [P, ZW])
        emb = sb("emb", [TYPES, GE])
        embT = sb("embT", [GE, TYPES])
        adw = sb("adw", [GE, GE])
        adwT = sb("adwT", [GE, GE])
        tt = sb("tt", [TYPES, 2 * GE])
        w1 = sb("w1", [D, R])
        w2 = sb("w2", [D, D])
        w3 = sb("w3", [D, 4, D])
        ps = [c.enter_context(nc.psum_tensor(f"ps{i}", [P, 4, 512], F32)) for i in range(2)]
        s_ms = sem("s_ms")
        s_ld = sem("s_ld")
        s_nodes = sem("s_nodes")
        s_con = sem("s_con")
        s_v = sem("s_v")
        s_tab = sem("s_tab")
        s_pe = sem("s_pe")
        s_a = sem("s_a")
        s_ep = sem("s_ep")
        s_tt = sem("s_tt")
        s_fin = sem("s_fin")
        s_z = sem("s_z")
        FT = FULL // P
        FR = FULL - FT * P
        cols = [(g("src_i"), S), (g("loc"), None), (g("loc_ns"), None), (g("exs"), None), (g("exs"), None),
                (g("cut"), None), (g("src_f"), None), (g("dst_i"), None)]

        block = c.enter_context(nc.Block())
        done, n_sin, n_exp = {}, [0], [0]

        @block.sync
        def _(sp):
            n = [0]

            def ld(dst, src):
                n[0] += 16
                sp.dma_start(dst, src).then_inc(s_ld if "edges" not in done else s_nodes, 16)

            sp.wait_ge(s_ms, 1)
            with nc.allow_non_contiguous_dma(reason="one element per chunk"):
                for tile, name in ((s_i, "src"), (d_i, "dst"), (LG, "edge_weight1"), (DIST, "edge_weight")):
                    v = a[name].rearrange("e o -> (e o)") if name == "edge_weight1" else a[name]
                    ld(tile[:, 0:FT, :], v[0:FT * P * P].rearrange("(k q p) -> q k p", q=P, p=P))
                    ld(tile[0:FR, FT, :], v[FT * P * P:FULL * P].rearrange("(q p) -> q p", p=P))
                    ld(tile[FR:FR + 1, FT, 0:REST], v[FULL * P:E].rearrange("(q p) -> q p", q=1))
                before = a["dst"][0:FULL * P].rearrange("(c p) -> c p", p=P)[:, P - 1:P]
                after = a["dst"][0:FULL * P].rearrange("(c p) -> c p", p=P)[:, 0:1]
                ld(pl_i[1:P, 0:1], before[0:P - 1, :])
                ld(pl_i[:, 1:FT], before[P - 1:P * FT - 1, :].rearrange("(k q) o -> q (k o)", q=P))
                ld(pl_i[0:FR + 1, FT:FT + 1], before[P * FT - 1:P * FT + FR, :])
                ld(nf_i[:, 0:FT], after[1:P * FT + 1, :].rearrange("(k q) o -> q (k o)", q=P))
                ld(nf_i[0:FR - 1, FT:FT + 1], after[P * FT + 1:P * FT + FR, :])
                ld(nf_i[FR - 1:FR, FT:FT + 1], a["dst"][FULL * P:FULL * P + 1].rearrange("(q p) -> q p", q=1))
            done["edges"], n[0] = n[0], 0
            for tile, name in ((X, "x"), (mult, "node_vec"), (z_i, "node_type_119")):
                v = a[name]
                if name == "x":
                    ld(tile[0:LAST_P, :, :], v[0:LAST_P * NB, :].rearrange("(p b) d -> p b d", b=NB))
                    ld(tile[LAST_P:LAST_P + 1, 0:LAST_B, :], v[LAST_P * NB:N, :].rearrange("(p b) d -> p b d", p=1))
                else:
                    ld(tile[0:LAST_P, :], v[0:LAST_P * NB].rearrange("(p b) -> p b", b=NB))
                    ld(tile[LAST_P:LAST_P + 1, 0:LAST_B], v[LAST_P * NB:N].rearrange("(p b) -> p b", p=1))
            ld(emb[:], a["L1_gnn_emb"])
            ld(adw[:], a["L1_gnn_adaptW"])
            ld(w1[:], a["L1_gnn_W1"])
            ld(w2[:], a["L1_gnn_W2"])
            ld(g("b1c")[:], a["L1_gnn_b1"].rearrange("(p o) -> p o", o=1))
            for t, nm in (("b2r", "L1_gnn_b2"), ("l2b1", "L2_gnn_b1"), ("l2b2", "L2_gnn_b2"), ("l3b", "L3_gnn_bias")):
                ld(g(t)[:], a[nm].rearrange("(p o) -> p o", p=1))
            for t, nm in (("gam", "L1_gnn_gamma"), ("bet", "L1_gnn_beta")):
                ld(g(t)[:], a[nm].rearrange("(p o) -> p o", p=1).to_broadcast([P, D]))
            for t, nm in (("wrel1", "L2_gnn_w_rel1"), ("wrel2", "L2_gnn_w_rel2"), ("wroot1", "L2_gnn_w_root1"),
                          ("wroot2", "L2_gnn_w_root2")):
                ld(g(t)[:], a[nm])
            ld(w3[:], a["L3_gnn_weight"].rearrange("k i o -> i k o"))
            done["all"] = n[0]
            z = 0
            for t, w in ((g("rank50"), D + 2), (g("rank48")[0], D), (g("rank48")[1], D), (g("rank48")[2], D),
                         (g("rank96"), 2 * D), (g("rank144"), 3 * D), *((t, D + 2) for t in g("scat"))):
                room = t[0:NP, :].rearrange("(p b) d -> p (b d)", b=NB)
                many = 4 * (w // D)
                sp.dma_start(room[:, 0:many * ZW].rearrange("p (r z) -> p r z", z=ZW),
                             zero[:].rearrange("p (o z) -> p o z", o=1).to_broadcast([P, many, ZW])).then_inc(s_z, 16)
                z += 16
                if w % D:
                    sp.dma_start(room[:, many * ZW:NB * w], zero[:, 0:NB * w - many * ZW]).then_inc(s_z, 16)
                    z += 16
            for t in g("scat"):
                sp.dma_start(t[NP:NP + P, :], zero[:, 0:D + 2]).then_inc(s_z, 16)
                z += 16
            sp.wait_ge(s_nodes, done["all"])
            sp.dma_start(node_rows(g("tab_in"), 0, D, 0), X[:]).then_inc(s_fin, 16)
            sp.wait_ge(s_tt, 1)
            sp.dma_start(g("tab_type")[:, :], tt[:]).then_inc(s_tab, 16)
            sp.wait_ge(s_ep, 16 * NB)
            sp.dma_start(node_rows(g("tab_in"), D, D + GE, 0), EP[:, :, 0:GE]).then_inc(s_fin, 16)
            sp.dma_start(node_rows(g("tab_dst"), D + 1, D + 1 + GE, 0), EP[:, :, GE:2 * GE]).then_inc(s_fin, 16)
            sp.wait_ge(s_fin, 48)
            sp.wait_ge(s_z, z)

        @block.gpsimd
        def _(pool):
            nc.gpsimd.memset(ident[:], 0.0).then_inc(s_con, 1)
            nc.gpsimd.memset(g("tril")[:], 1.0).then_inc(s_con, 1)
            pool.wait_ge(s_con, 2)
            nc.gpsimd.affine_select(out=ident[:], in_=ident[:], compare_op=ALU.not_equal, fill=1.0, base=0,
                                    pattern=[[-1, P]], channel_multiplier=1).then_inc(s_con, 1)
            nc.gpsimd.affine_select(out=g("tril")[:], in_=g("tril")[:], compare_op=ALU.is_gt, fill=0.0, base=0,
                                    pattern=[[-1, P]], channel_multiplier=1).then_inc(s_con, 1)
            nc.gpsimd.iota(g("iota_row")[:], pattern=[[1, P]], base=0, channel_multiplier=0,
                           allow_small_or_imprecise_dtypes=True).then_inc(s_con, 1)
            nc.gpsimd.iota(g("spare_id")[:], pattern=[[1, 1]], base=NP, channel_multiplier=1,
                           allow_small_or_imprecise_dtypes=True).then_inc(s_con, 1)
            pool.wait_ge(s_tab, 16)
            pool.wait_ge(s_nodes, done["all"])
            for b in range(NB):
                nc.gpsimd.indirect_dma_start(
                    out=EP[:, b, :], out_offset=None, in_=g("tab_type")[:, :],
                    in_offset=bass.IndirectOffsetOnAxis(ap=z_i[:, b:b + 1], axis=0)).then_inc(s_ep, 16)
            pool.wait_ge(s_ep, 16 * NB)

        steps = []

        @block.vector
        def _(dve):
            n = [0]

            def v(ins):
                n[0] += 1
                ins.then_inc(s_v, 1)
                dve.wait_ge(s_v, n[0])

            def ask_pe(fn):
                steps.append((n[0], fn))
                dve.wait_ge(s_pe, len(steps))

            V3 = nc.vector
            for t, val in ((s_i, 0), (d_i, PAD_DST), (pl_i, PAD_DST), (nf_i, PAD_DST), (LG, 0.0), (DIST, 0.0),
                           (X, 0.0), (mult, 0.0), (z_i, 0), (g("exs"), 0.0)):
                V3.memset(t[:], val)
            V3.memset(g("loc")[:], -1.0)
            V3.memset(g("loc_ns")[:], -1.0)
            V3.memset(zero[:], 0.0)
            V3.memset(g("ones_row")[:], 1.0)
            V3.memset(halfpi[:], 1.5707963267948966)
            v(V3.memset(g("eps_c")[:], EPS))
            v(V3.memset(PR[:], 1.0))
            V3.memset(PR[:, :, 0:1], 0.0).then_inc(s_ms, 1)
            v(V3.memset(pl_i[0:1, 0:1], -1))
            dve.wait_ge(s_ms, 1)
            dve.wait_ge(s_ld, done["edges"])
            V3.tensor_copy(S[:], s_i[:])
            V3.tensor_copy(pl[:], pl_i[:])
            V3.tensor_copy(nf[:], nf_i[:])
            v(V3.tensor_copy(Dd[:], d_i[:]))
            V3.tensor_tensor(F[:, :, 1:P], Dd[:, :, 1:P], Dd[:, :, 0:P - 1], ALU.not_equal)
            V3.tensor_tensor(F[:, :, 0], Dd[:, :, 0], pl[:], ALU.not_equal)
            v(V3.tensor_scalar(V[:], Dd[:], float(PAD_DST - 1), None, ALU.is_lt))
            v(V3.tensor_tensor_scan(out=T1.rearrange("p k q -> p (k q)"), data0=PR[:].rearrange("p k q -> p (k q)"),
                                    data1=F[:].rearrange("p k q -> p (k q)"), initial=0.0, op0=ALU.mult, op1=ALU.add))
            V3.tensor_copy(col[0][:], T1[:, :, P - 1])
            v(V3.tensor_tensor(Mx, T1, F[:, :, 0:1].to_broadcast([P, KT, P]), ALU.subtract))
            V3.tensor_copy(col[1][:], F[:, :, 0])
            v(V3.scalar_tensor_tensor(out=Q[:].rearrange("p k q -> p (k q)"), in0=Mx.rearrange("p k q -> p (k q)"),
                                      scalar=1.0, in1=V[:].rearrange("p k q -> p (k q)"), op0=ALU.add, op1=ALU.mult))
            v(V3.tensor_scalar(T1, Q[:], -1.0, None, ALU.add))

            def to_cols(src, dst, w=CHUNKS, conv=None):
                buf = ps[0]

                def pe(e):
                    for k in range(KT):
                        ins = nc.tensor.transpose(buf[:, k // 4, (k % 4) * P:(k % 4 + 1) * P], src[:, k, :], ident[:])
                    return ins
                ask_pe(pe)
                v(V3.tensor_copy(dst, buf[:].rearrange("p a b -> p (a b)")[:, 0:w]))

            to_cols(S, g("src_i")[:])
            to_cols(T1, g("loc")[:, 0:CHUNKS])
            v(V3.tensor_tensor(Mx, S[:], Dd[:], ALU.not_equal))
            v(V3.tensor_tensor(Q[:], Q[:], Mx, ALU.mult))
            v(V3.tensor_scalar(Q[:], Q[:], -1.0, None, ALU.add))
            to_cols(Q, g("loc_ns")[:, 0:CHUNKS])
            v(V3.scalar_tensor_tensor(out=Q[:].rearrange("p k q -> p (k q)"), in0=Dd[:].rearrange("p k q -> p (k q)"),
                                      scalar=1.0, in1=V[:].rearrange("p k q -> p (k q)"), op0=ALU.add, op1=ALU.mult))
            v(V3.tensor_tensor(Q[:], Q[:], F[:], ALU.mult))
            to_cols(Q, g("exs")[:, 0:CHUNKS, 1])
            v(V3.tensor_tensor(Q[:], Dd[:], V[:], ALU.mult))
            to_cols(Q, g("dst_i")[:])
            v(V3.tensor_scalar(Q[:], V[:], -float(PAD_DST), float(PAD_DST), ALU.mult, ALU.add))
            v(V3.tensor_tensor(Q[:], Q[:], S[:], ALU.add))
            to_cols(Q, g("src_f")[:])
            v(V3.tensor_scalar(DIST[:], DIST[:], 6.0, None, ALU.min))
            n_sin[0] = n[0]
            dve.wait_ge(s_a, 1)
            v(V3.tensor_tensor(DIST[:], DIST[:], DIST[:], ALU.mult))
            to_cols(DIST, g("cut")[:])

            def to_row(src, dst):
                buf = ps[1]

                def pe(e):
                    for k in range(KT):
                        ins = nc.tensor.matmul(buf[0:1, k // 4, (k % 4) * P:(k % 4 + 1) * P], src[:, k:k + 1], ident[:],
                                               start=True, stop=True)
                    return ins
                ask_pe(pe)
                v(V3.tensor_copy(dst, buf[0:1, :, :].rearrange("p a b -> p (a b)")[:, 0:ROWS]))

            def from_row(src, dst):
                buf = ps[1]

                def pe(e):
                    for k in range(KT):
                        ins = nc.tensor.matmul(buf[:, 0, k:k + 1], src[0:1, k * P:(k + 1) * P], g("ones_row")[0:1, 0:1],
                                               start=True, stop=True)
                    return ins
                ask_pe(pe)
                v(V3.tensor_copy(dst[:], buf[:, 0, 0:KT]))

            to_row(col[0], rows[0])
            to_row(col[1], rows[1])
            v(V3.memset(rows[3], 0.0))
            v(V3.tensor_tensor_scan(out=rows[2], data0=rows[3], data1=rows[0], initial=0.0, op0=ALU.add, op1=ALU.add))
            v(V3.tensor_tensor(rows[2], rows[2], rows[0], ALU.subtract))
            v(V3.tensor_tensor(rows[2], rows[2], rows[1], ALU.add))
            v(V3.tensor_scalar(g("win_row")[:], rows[2], -1.0, None, ALU.add))

            flat = lambda t: t[:, :, :].rearrange("p k q -> p (k q)")
            ends = T1
            V3.tensor_copy(ends[:, :, 0:P - 1], F[:, :, 1:P])
            v(V3.tensor_tensor(ends[:, :, P - 1], Dd[:, :, P - 1], nf[:], ALU.not_equal))
            v(V3.tensor_reduce(col[0][:], F[:], AX.X, ALU.max))
            v(V3.tensor_reduce(col[1][:], ends[:], AX.X, ALU.max))
            for t in (F, ends, col[0], col[1]):
                w = t if t is T1 else t[:]
                v(V3.tensor_scalar(w, w, -2.0 * BIG, BIG, ALU.mult, ALU.add))
            for rev, guard, hs, edge, tail, vals in ((False, F, col[0], 0, P - 1, LG), (True, ends, col[1], P - 1, 0, Mx)):
                fl = (lambda x: x[:, ::-1]) if rev else (lambda x: x)
                v(V3.tensor_copy(col[2][:], guard[:, :, edge]))
                v(V3.memset(guard[:, :, edge:edge + 1], -BIG))
                if not rev:
                    v(V3.tensor_copy(Q[:], LG[:]))
                    src_t = Q
                else:
                    src_t = Q
                v(V3.tensor_tensor_scan(out=fl(flat(Mx)), data0=fl(flat(guard)), data1=fl(flat(src_t)), initial=-BIG,
                                        op0=ALU.min, op1=ALU.max))
                v(V3.tensor_copy(col[3][:], Mx[:, :, tail]))
                to_row(col[3], rows[0])
                to_row(hs, rows[1])
                v(V3.tensor_tensor_scan(out=fl(rows[2]), data0=fl(rows[1]), data1=fl(rows[0]), initial=-BIG,
                                        op0=ALU.min, op1=ALU.max))
                v(V3.memset(rows[3], -BIG))
                if rev:
                    v(V3.tensor_copy(rows[3][:, 0:ROWS - 1], rows[2][:, 1:ROWS]))
                else:
                    v(V3.tensor_copy(rows[3][:, 1:ROWS], rows[2][:, 0:ROWS - 1]))
                from_row(rows[3], car)
                v(V3.tensor_tensor(car[:], car[:], col[2][:], ALU.min))
                v(V3.tensor_tensor(src_t[:, :, edge], src_t[:, :, edge], car[:], ALU.max))
                v(V3.tensor_tensor_scan(out=fl(flat(Mx)), data0=fl(flat(guard)), data1=fl(flat(src_t)), initial=-BIG,
                                        op0=ALU.min, op1=ALU.max))
                if not rev:
                    v(V3.tensor_copy(Q[:], Mx))
            v(V3.tensor_tensor(LG[:], LG[:], Mx, ALU.subtract))
            n_exp[0] = n[0]
            dve.wait_ge(s_a, 2)
            v(V3.tensor_copy(LG[:], LG[:]))
            to_cols(LG, g("exs")[:, 0:CHUNKS, 0])

            dve.wait_ge(s_nodes, done["all"])
            v(V3.memset(col[4][:], 0.0))

            def small(src, dst, m, k):
                buf = ps[0]
                ask_pe(lambda e: nc.tensor.transpose(buf[0:m, 0, 0:k], src, ident[0:k, 0:k]))
                v(V3.tensor_copy(dst, buf[0:m, 0, 0:k]))

            small(emb[:], embT[:], GE, TYPES)
            small(adw[:], adwT[:], GE, GE)
            ask_pe(lambda e: nc.tensor.matmul(ps[0][0:TYPES, 0, 0:GE], embT[:], adwT[:], start=True, stop=True))
            V3.tensor_copy(tt[:, 0:GE], emb[:])
            v(V3.tensor_copy(tt[:, GE:2 * GE], ps[0][0:TYPES, 0, 0:GE]))
            V3.memset(col[5][:], 0.0).then_inc(s_tt, 1)
            small(w1[:], g("w1T")[:], R, D)
            small(w2[:], g("w2T")[:], D, D)
            V3.tensor_copy(g("id50")[:], ident[0:D + 2, 0:D + 2])
            V3.tensor_copy(g("w3i13")[:, 0:D], ident[0:D, 0:D])
            V3.tensor_copy(g("w3i13")[:, D:2 * D], w3[:, 1, :])
            V3.tensor_copy(g("w3i13")[:, 2 * D:3 * D], w3[:, 3, :])
            V3.tensor_copy(g("w3i2")[:, 0:D], ident[0:D, 0:D])
            V3.tensor_copy(g("w3i2")[:, D:2 * D], w3[:, 2, :])
            v(V3.tensor_tensor(g("w302")[:], w3[:, 0, :], w3[:, 2, :], ALU.subtract))

        @block.scalar
        def _(act):
            act.wait_ge(s_v, n_sin[0])
            nc.scalar.activation(DIST[:], DIST[:], ACT.Sin, bias=halfpi[:], scale=-3.141592653589793 / 12).then_inc(s_a, 1)
            act.wait_ge(s_v, n_exp[0])
            nc.scalar.activation(LG[:], LG[:], ACT.Exp).then_inc(s_a, 1)

        @block.tensor
        def _(pe):
            pe.wait_ge(s_con, 6)
            for n_v, fn in steps:
                pe.wait_ge(s_v, n_v)
                fn(pe).then_inc(s_pe, 1)


def cleared(nc, c, role):
    if role not in ROLES:
        ROLES[role] = nc.alloc_semaphore(role)
    else:
        CLEAR.append(ROLES[role])
    return ROLES[role]


ROLES = {}
CLEAR = []


def clear_all(nc):
    if not CLEAR:
        return
    with nc.Block() as block:
        @block.gpsimd
        def _(pool):
            low, high = min(s.num for s in CLEAR), max(s.num for s in CLEAR) + 1
            nc.gpsimd.dma_reset(range(low, high))
            for s in CLEAR:
                nc.gpsimd.sem_clear(s)
    CLEAR.clear()


def gather_pass(nc, L, name, table, width, loc, weights=False, emb_edge=None, dense=None, dense_in="X"):
    arena, iota_row, X, OUT = L["arena"], L["iota_row"], L["X"], L["OUT"]
    DI = L[dense_in]
    exs, src_i, win_row, ident, ones_row = L["exs"], L["src_i"], L["win_row"], L["ident"], L["ones_row"]
    M = D + 2 if weights else D
    with ExitStack() as c:
        def sb(nm, shape, dt=F32):
            return c.enter_context(nc.sbuf_tensor(f"{name}_{nm}", shape, dt))

        def sem(nm):
            return cleared(nc, c, f"pass_{nm}")
        idx = sb("idx", [P, UI, UG], I32)
        rows = sb("rows", [P, UI, UG, width])
        hot = sb("hot", [P, 2, UG, P])
        msg = sb("msg", [P, 2, UG, M]) if weights else None
        xs = sb("xs", [P, D])
        xT = sb("xT", [D, P])
        win = c.enter_context(nc.psum_tensor(f"{name}_win", [D + 2, 2, UG, P], F32))
        dt_ps = c.enter_context(nc.psum_tensor(f"{name}_dt", [D, P], F32))
        do_ps = c.enter_context(nc.psum_tensor(f"{name}_do", [P, D], F32))
        s_idx = sem("idx_staged")
        s_rows = [sem(f"rows_landed{i}") for i in range(UI)]
        s_hot = sem("onehot_built")
        s_msg = sem("messages_built")
        s_win = sem("window_summed")
        s_acc = sem("window_added")
        s_emb = [sem(f"embeddings_stored{i}") for i in range(UI)] if weights else None
        s_xs = sem("block_staged")
        s_dt = sem("block_turned")
        s_xT = sem("turned_copied")
        s_do = sem("block_multiplied")
        s_out = sem("block_out")
        clear_all(nc)
        block = c.enter_context(nc.Block())

        @block.gpsimd
        def _(pool):
            def step(it, first, last):
                for s in range(UI):
                    pool.wait_ge(s_idx, it * UI + (s + 1))
                    if not first:
                        if weights:
                            pool.wait_ge(s_msg, it * UI + (s - UI + 1))
                            pool.wait_ge(s_emb[s], it * 16)
                        else:
                            pool.wait_ge(s_win, it * UI + (s - UI + 1))
                    nc.gpsimd.nop(nofuse=True)
                    for j in range(UG):
                        nc.gpsimd.indirect_dma_start(
                            out=rows[:, s, j, :], out_offset=None, in_=table[:, :],
                            in_offset=bass.IndirectOffsetOnAxis(ap=idx[:, s, j:j + 1], axis=0)).then_inc(s_rows[s], 16)
            run_steps(nc.gpsimd, step)
            for s in range(UI):
                pool.wait_ge(s_rows[s], 16 * UG * STEPS)

        if weights:
            @block.sync
            def _(sp):
                store = emb_edge.rearrange("(g j p) d -> p g j d", j=UG, p=P)

                def step(it, first, last):
                    for s in range(UI):
                        sp.wait_ge(s_rows[s], it * (16 * UG) + 16 * UG)
                        nc.sync.nop(nofuse=True)
                        sp.dma_start(store[:, bass.ds(it * UI + s, 1), :, :].rearrange("p g j d -> p (g j) d"),
                                     rows[:, s, :, D:D + GE]).then_inc(s_emb[s], 16)
                run_steps(nc.sync, step)
                for s in range(UI):
                    sp.wait_ge(s_emb[s], 16 * STEPS)

        @block.scalar
        def _(act):
            def stage(it, s):
                nc.scalar.copy(idx[:, s, :], src_i[:, bass.ds((it * UI + s) * UG, UG)]).then_inc(s_idx, 1)

            for s in range(UI):
                stage(0, s)

            def step(it, first, last):
                if dense:
                    if not first:
                        act.wait_ge(s_dt, it)
                    nc.scalar.copy(xs[:], DI[:, bass.ds(it, 1), :].rearrange("p o d -> p (o d)")).then_inc(s_xs, 1)
                for s in range(UI):
                    if not last:
                        act.wait_ge(s_rows[s], it * (16 * UG) + 16 * UG)
                        stage(it + 1, s)
                    if dense and s == 1:
                        act.wait_ge(s_dt, it + 1)
                        if not first:
                            act.wait_ge(s_do, it)
                        nc.scalar.copy(xT[:], dt_ps[:]).then_inc(s_xT, 1)
                    if dense and s == 3:
                        act.wait_ge(s_do, it + 1)
                        nc.scalar.copy(OUT[:, bass.ds(it, 1), :].rearrange("p o d -> p (o d)"),
                                       do_ps[:]).then_inc(s_out, 1)
            run_steps(nc.scalar, step)

        @block.vector
        def _(dve):
            nc.vector.memset(arena[0:M, :], 0.0).then_inc(s_acc, 1)
            dve.wait_ge(s_acc, 1)

            def build(it, s):
                nx, b = s % UI, s % 2
                if not (isinstance(it, int) and it * UI + s < 2):
                    dve.wait_ge(s_win, it * UI + (s - 1))
                nc.vector.tensor_tensor(
                    hot[:, b, :, :], iota_row[:].rearrange("p (o q) -> p o q", o=1).to_broadcast([P, UG, P]),
                    loc[:, bass.ds((it * UI + s) * UG, UG)].rearrange("p (g o) -> p g o", o=1).to_broadcast([P, UG, P]),
                    ALU.is_equal).then_inc(s_hot, 1)
                if weights:
                    e = exs[:, bass.ds((it * UI + s) * UG, UG), :]
                    wait_it = it if s < UI else it + 1
                    dve.wait_ge(s_rows[nx], wait_it * (16 * UG) + 16 * UG)
                    nc.vector.tensor_copy(msg[:, b, :, D:D + 2], e)
                    nc.vector.tensor_tensor(msg[:, b, :, 0:D], rows[:, nx, :, 0:D],
                                            e[:, :, 0:1].to_broadcast([P, UG, D]), ALU.mult).then_inc(s_msg, 1)

            build(0, 0)

            def step(it, first, last):
                for s in range(UI):
                    if not (last and s == UI - 1):
                        build(it, s + 1)
                    _, at = nc.values_load_multi_w_load_instructions(
                        win_row[0:1, bass.ds((it * UI + s) * UG, UG)], engines=[mybir.EngineType.DVE],
                        min_val=0, max_val=NP)
                    dve.wait_ge(s_win, it * UI + (s + 1))
                    for j in range(UG):
                        into = arena[0:M, bass.ds(at[j], P)]
                        nc.vector.tensor_tensor(into, into, win[0:M, s % 2, j, :], ALU.add).then_inc(s_acc, 1)
                        dve.wait_ge(s_acc, (it * UI + s) * UG + (j + 2))
            run_steps(nc.vector, step)

        @block.tensor
        def _(pe):
            def step(it, first, last):
                for s in range(UI):
                    b = s % 2
                    pe.wait_ge(s_hot, it * UI + (s + 1))
                    if weights:
                        pe.wait_ge(s_msg, it * UI + (s + 1))
                    else:
                        pe.wait_ge(s_rows[s], it * (16 * UG) + 16 * UG)
                    if not (first and s < 2):
                        pe.wait_ge(s_acc, (it * UI + s - 1) * UG + 1)
                    nc.tensor.nop(nofuse=True)
                    for j in range(UG):
                        ins = nc.tensor.matmul(win[0:M, b, j, :], msg[:, b, j, :] if weights else rows[:, s, j, :],
                                               hot[:, b, j, :], start=True, stop=True)
                    ins.then_inc(s_win, 1)
                    if dense and s == 1:
                        pe.wait_ge(s_xs, it + 1)
                        if not first:
                            pe.wait_ge(s_xT, it)
                        nc.tensor.nop(nofuse=True)
                        nc.tensor.transpose(dt_ps[:], xs[:], ident[:]).then_inc(s_dt, 1)
                    if dense and s == 3:
                        pe.wait_ge(s_xT, it + 1)
                        if not first:
                            pe.wait_ge(s_out, it)
                        nc.tensor.nop(nofuse=True)
                        nc.tensor.matmul(do_ps[:], ones_row[:], dense[1][:], start=True, stop=False)
                        nc.tensor.matmul(do_ps[:], xT[:], dense[0][:], start=False, stop=True).then_inc(s_do, 1)
            run_steps(nc.tensor, step)


def rank_nodes(nc, L):
    arena, id50, node_idx, stat = L["arena"], L["id50"], L["node_idx"], L["stat"]
    with ExitStack() as c:
        nd = c.enter_context(nc.psum_tensor("rn_ps", [P, NB], F32))
        rid = c.enter_context(nc.sbuf_tensor("rn_id", [P, NB], F32))
        s_pe = cleared(nc, c, "rn_turned")
        s_v = cleared(nc, c, "rn_dve")
        s_io = cleared(nc, c, "rn_iota")
        clear_all(nc)
        block = c.enter_context(nc.Block())

        @block.gpsimd
        def _(pool):
            nc.gpsimd.iota(rid[:], pattern=[[P, NB]], base=NP + 1, channel_multiplier=1,
                           allow_small_or_imprecise_dtypes=True).then_inc(s_io, 1)

        @block.tensor
        def _(pe):
            for b in range(NB):
                ins = nc.tensor.matmul(nd[:, b:b + 1], arena[0:D + 2, b * P:(b + 1) * P], id50[:, D + 1:D + 2],
                                       start=True, stop=True)
            ins.then_inc(s_pe, 1)

        @block.vector
        def _(dve):
            dve.wait_ge(s_pe, 1)
            dve.wait_ge(s_io, 1)
            nc.vector.tensor_scalar(stat[0][:], nd[:], 0.5, None, ALU.is_lt).then_inc(s_v, 1)
            dve.wait_ge(s_v, 1)
            nc.vector.tensor_tensor(stat[0][:], stat[0][:], rid[:], ALU.mult).then_inc(s_v, 1)
            dve.wait_ge(s_v, 2)
            nc.vector.scalar_tensor_tensor(out=node_idx[:], in0=nd[:], scalar=-1.0, in1=stat[0][:],
                                           op0=ALU.add, op1=ALU.add).then_inc(s_v, 1)


def rank_rows(nc, L, name, mat, K, W, table):
    arena, node_idx = L["arena"], L["node_idx"]
    with ExitStack() as c:
        def sb(nm, shape, dt=F32):
            return c.enter_context(nc.sbuf_tensor(f"{name}_{nm}", shape, dt))

        def sem(nm):
            return cleared(nc, c, f"ranks_{nm}")
        blk = sb("blk", [D + 2, 2, RB, P])
        idx = sb("idx", [P, 2, RB], I32)
        rows = sb("rows", [P, 2, RB, W])
        ps = [c.enter_context(nc.psum_tensor(f"{name}_ps{i}", [P, RB, 256], F32)) for i in range(2)]
        s_blk = sem("blocks_staged")
        s_idx = sem("idx_staged")
        s_ps = sem("blocks_multiplied")
        s_rows = sem("rows_copied")
        s_put = [sem(f"rows_stored{i}") for i in range(2)]
        clear_all(nc)
        block = c.enter_context(nc.Block())

        def steps(engine, body):
            body(0, True)
            with engine.Fori(1, RSTEPS) as it:
                body(it, False)

        @block.scalar
        def _(act):
            def step(it, first):
                for s in range(2):
                    if not first:
                        act.wait_ge(s_ps, it * 2 + (s - 1))
                        act.wait_ge(s_put[s], it * (16 * RB))
                    nc.scalar.copy(blk[0:K, s, :, :].rearrange("k r p -> k (r p)"),
                                   arena[0:K, bass.ds((it * 2 + s) * (RB * P), RB * P)]).then_inc(s_blk, 1)
                    nc.scalar.copy(idx[:, s, :], node_idx[:, bass.ds((it * 2 + s) * RB, RB)]).then_inc(s_idx, 1)
            steps(nc.scalar, step)

        @block.tensor
        def _(pe):
            def step(it, first):
                for s in range(2):
                    pe.wait_ge(s_blk, it * 2 + (s + 1))
                    if not first:
                        pe.wait_ge(s_rows, it * 2 + (s - 1))
                    nc.tensor.nop(nofuse=True)
                    for r in range(RB):
                        ins = nc.tensor.matmul(ps[s][:, r, 0:W], blk[0:K, s, r, :], mat[0:K, 0:W], start=True, stop=True)
                    ins.then_inc(s_ps, 1)
            steps(nc.tensor, step)

        @block.vector
        def _(dve):
            def step(it, first):
                for s in range(2):
                    dve.wait_ge(s_ps, it * 2 + (s + 1))
                    if not first:
                        dve.wait_ge(s_put[s], it * (16 * RB))
                    nc.vector.tensor_copy(rows[:, s, :, :], ps[s][:, :, 0:W]).then_inc(s_rows, 1)
            steps(nc.vector, step)

        @block.gpsimd
        def _(pool):
            def step(it, first):
                for s in range(2):
                    pool.wait_ge(s_rows, it * 2 + (s + 1))
                    pool.wait_ge(s_idx, it * 2 + (s + 1))
                    nc.gpsimd.nop(nofuse=True)
                    for r in range(RB):
                        nc.gpsimd.indirect_dma_start(
                            out=table[:, :], out_offset=bass.IndirectOffsetOnAxis(ap=idx[:, s, r:r + 1], axis=0),
                            in_=rows[:, s, r, :], in_offset=None).then_inc(s_put[s], 16)
            steps(nc.gpsimd, step)
            for s in range(2):
                pool.wait_ge(s_put[s], 16 * RB * RSTEPS)


class NodePhase:

    def __init__(self, nc, L, name, loads, stores, compute):
        with ExitStack() as c:
            s_ld = cleared(nc, c, "nodes_loaded")
            s_v = cleared(nc, c, "nodes_dve")
            s_a = cleared(nc, c, "nodes_act")
            s_st = cleared(nc, c, "nodes_stored")
            clear_all(nc)
            block = c.enter_context(nc.Block())
            asks, ready = [], {}

            @block.vector
            def _(dve):
                n = [0]

                def v(ins):
                    n[0] += 1
                    ins.then_inc(s_v, 1)
                    dve.wait_ge(s_v, n[0])

                def act(fn):
                    asks.append((n[0], fn))
                    dve.wait_ge(s_a, len(asks))

                def loaded(i):
                    dve.wait_ge(s_ld, 16 * (i + 1))

                def free(i):
                    ready[i] = n[0]
                compute(nc, v, act, loaded, free)
                ready["end"] = n[0]

            @block.scalar
            def _(act):
                for at, fn in asks:
                    act.wait_ge(s_v, at)
                    fn().then_inc(s_a, 1)

            @block.sync
            def _(sp):
                for i, (dst, src) in enumerate(loads):
                    if i in ready:
                        sp.wait_ge(s_v, ready[i])
                    if i:
                        sp.wait_ge(s_ld, 16 * i)
                    sp.dma_start(dst, src).then_inc(s_ld, 16)
                sp.wait_ge(s_v, ready["end"])
                for dst, src in stores:
                    sp.dma_start(dst, src).then_inc(s_st, 16)
                sp.wait_ge(s_st, 16 * len(stores))


def bc(t):
    return t.rearrange("p (b o) -> p b o", o=1).to_broadcast([P, NB, D])


def layernorm(nc, v, act, L, dst, tmp, src):
    m, r = L["stat"][0][:], L["stat"][1][:]
    V = nc.vector
    v(V.tensor_reduce(m, src, AX.X, ALU.add))
    v(V.tensor_scalar(m, m, 1.0 / D, None, ALU.mult))
    v(V.tensor_tensor(dst, src, bc(m), ALU.subtract))
    v(V.tensor_tensor(tmp, dst, dst, ALU.mult))
    v(V.tensor_reduce(r, tmp, AX.X, ALU.add))
    act(lambda: nc.scalar.activation(r, r, ACT.Sqrt, bias=L["eps_c"][:], scale=1.0 / D))
    v(V.reciprocal(r, r))
    v(V.tensor_tensor(dst, dst, bc(r), ALU.mult))


def room(L, at, width, blocks=NB):
    return L["arena"][:, at:at + blocks * width].rearrange("p (b d) -> p b d", d=width)


def nodes0(nc, L):
    A, X, TMP, OUT, st = room(L, 0, D + 2), L["X"][:], L["TMP"][:], L["OUT"][:], L["stat"]

    def compute(nc, v, act, loaded, free):
        V = nc.vector
        loaded(0)
        v(V.tensor_scalar(st[0][:], A[:, :, D], 0.5, None, ALU.max))
        v(V.reciprocal(st[0][:], st[0][:]))
        v(V.tensor_tensor(TMP, A[:, :, 0:D], bc(st[0][:]), ALU.mult))
        v(V.tensor_scalar(OUT, TMP, 0.0, None, ALU.min))
        act(lambda: nc.scalar.activation(OUT, OUT, ACT.Exp))
        v(V.tensor_scalar(TMP, TMP, 0.0, -1.0, ALU.max, ALU.add))
        v(V.tensor_tensor(TMP, TMP, OUT, ALU.add))
        v(V.tensor_tensor(TMP, TMP, X, ALU.add))
        layernorm(nc, v, act, L, X, OUT, TMP)
        v(V.tensor_tensor(TMP, X, bc(L["mult"][:]), ALU.mult))
    with nc.allow_non_contiguous_dma(reason="one column of the table"):
        NodePhase(nc, L, "n0", [(A, node_rows(L["rank50"], 0, D + 2, 0))],
                  [(node_rows(L["tab_dst"], 0, D, 0), TMP),
                   (node_rows(L["tab_dst"], D, D + 1, 0), L["mult"][:].rearrange("p (b o) -> p b o", o=1))], compute)


def nodes1(nc, L):
    W = D + 2
    A, B, X, TMP, OUT, st = room(L, 0, W), room(L, NB * W, W), L["X"][:], L["TMP"][:], L["OUT"][:], L["stat"]
    dis = L["dis"][:]

    def rows(i):
        return L["scat"][i][0:NP, :].rearrange("(p b) d -> p b d", b=NB)

    def compute(nc, v, act, loaded, free):
        V = nc.vector
        loaded(0)
        for i in range(1, UG):
            loaded(i)
            v(V.tensor_tensor(A, A, B, ALU.add))
            free(i + 1)
        v(V.tensor_scalar(st[0][:], A[:, :, D], 1e-8, None, ALU.max))
        v(V.reciprocal(st[0][:], st[0][:]))
        v(V.tensor_tensor(TMP, A[:, :, 0:D], bc(st[0][:]), ALU.mult))
        v(V.tensor_tensor(TMP, TMP, X, ALU.add))
        v(V.tensor_scalar(dis, A[:, :, D + 1], 0.5, None, ALU.max))
        act(lambda: nc.scalar.activation(dis, dis, ACT.Sqrt))
        v(V.reciprocal(dis, dis))
        v(V.tensor_scalar(st[0][:], A[:, :, D + 1], 0.5, None, ALU.is_gt))
        v(V.tensor_tensor(dis, dis, st[0][:], ALU.mult))
        layernorm(nc, v, act, L, OUT, room(L, 0, D), TMP)
        g = L["gam"][:].rearrange("p (o d) -> p o d", o=1).to_broadcast([P, NB, D])
        b = L["bet"][:].rearrange("p (o d) -> p o d", o=1).to_broadcast([P, NB, D])
        v(V.tensor_tensor(OUT, OUT, g, ALU.mult))
        v(V.tensor_tensor(OUT, OUT, b, ALU.add))
        v(V.tensor_tensor(OUT, OUT, X, ALU.add))
        layernorm(nc, v, act, L, X, TMP, OUT)
    NodePhase(nc, L, "n1", [(A, rows(0))] + [(B, rows(i)) for i in range(1, UG)],
              [(node_rows(L["tab_h"][0], 0, D, 0), X)], compute)


def nodes2a(nc, L):
    A, TMP, OUT = room(L, 0, D), L["TMP"][:], L["OUT"][:]

    def compute(nc, v, act, loaded, free):
        loaded(0)
        v(nc.vector.tensor_tensor(TMP, A, OUT, ALU.add))
        v(nc.vector.tensor_scalar(TMP, TMP, 0.0, None, ALU.max))
    NodePhase(nc, L, "n2a", [(A, node_rows(L["rank48"][0], 0, D, 0))], [(node_rows(L["tab_h"][1], 0, D, 0), TMP)],
              compute)


def nodes2b(nc, L):
    A, X, TMP, OUT = room(L, 0, D), L["X"][:], L["TMP"][:], L["OUT"][:]

    def compute(nc, v, act, loaded, free):
        V = nc.vector
        loaded(0)
        v(V.tensor_tensor(TMP, A, OUT, ALU.add))
        v(V.tensor_tensor(TMP, TMP, X, ALU.add))
        layernorm(nc, v, act, L, X, OUT, TMP)
        v(V.tensor_tensor(TMP, X, bc(L["dis"][:]), ALU.mult))
    NodePhase(nc, L, "n2b", [(A, node_rows(L["rank48"][1], 0, D, 0))], [(node_rows(L["tab_h"][2], 0, D, 0), TMP)],
              compute)


def nodes3a(nc, L):
    H = NB // 2
    A = room(L, 0, 3 * D, H)
    OUT, TMP = L["OUT"], L["TMP"]
    dis, d2 = L["dis"][:], L["stat"][0][:]

    def compute(nc, v, act, loaded, free):
        V = nc.vector
        v(V.tensor_tensor(d2, dis, dis, ALU.mult))
        for h in range(2):
            loaded(h)
            o, t = OUT[:, h * H:(h + 1) * H, :], TMP[:, h * H:(h + 1) * H, :]
            dh = dis[:, h * H:(h + 1) * H].rearrange("p (b o) -> p b o", o=1).to_broadcast([P, H, D])
            d2h = d2[:, h * H:(h + 1) * H].rearrange("p (b o) -> p b o", o=1).to_broadcast([P, H, D])
            v(V.tensor_tensor(t, A[:, :, 2 * D:3 * D], A[:, :, D:2 * D], ALU.subtract))
            v(V.tensor_tensor(t, t, dh, ALU.mult))
            v(V.tensor_tensor(o, o, t, ALU.add))
            v(V.scalar_tensor_tensor(out=t, in0=A[:, :, 0:D], scalar=-1.0, in1=d2h, op0=ALU.mult, op1=ALU.mult))
            free(h + 1)
    r = L["rank144"]
    NodePhase(nc, L, "n3a", [(A, node_rows(r, 0, 0, 0)) if False else (A, r[0:NP, :].rearrange("(p b) d -> p b d", b=NB)[:, h * H:(h + 1) * H, :]) for h in range(2)],
              [(node_rows(L["tab_h"][3], 0, D, 0), TMP[:])], compute)


def nodes3b(nc, L):
    A, X, TMP, OUT = room(L, 0, 2 * D), L["X"][:], L["TMP"][:], L["OUT"][:]
    dis = bc(L["dis"][:])

    def compute(nc, v, act, loaded, free):
        V = nc.vector
        loaded(0)
        v(V.scalar_tensor_tensor(out=TMP, in0=A[:, :, D:2 * D], scalar=-2.0, in1=dis, op0=ALU.mult, op1=ALU.mult))
        v(V.tensor_tensor(OUT, OUT, TMP, ALU.add))
        v(V.scalar_tensor_tensor(out=TMP, in0=A[:, :, 0:D], scalar=-2.0, in1=dis, op0=ALU.mult, op1=ALU.mult))
        v(V.tensor_tensor(TMP, TMP, X, ALU.subtract))
        v(V.tensor_tensor(TMP, TMP, dis, ALU.mult))
    NodePhase(nc, L, "n3b", [(A, node_rows(L["rank96"], 0, 2 * D, 0))], [(node_rows(L["tab_h"][4], 0, D, 0), TMP)],
              compute)


def nodes3c(nc, L, out):
    A, X, TMP, OUT = room(L, 0, D), L["X"][:], L["TMP"], L["OUT"][:]
    T = TMP[:]

    def compute(nc, v, act, loaded, free):
        V = nc.vector
        loaded(0)
        v(V.scalar_tensor_tensor(out=T, in0=A, scalar=-2.0, in1=bc(L["dis"][:]), op0=ALU.mult, op1=ALU.mult))
        v(V.tensor_tensor(T, T, OUT, ALU.add))
        v(V.tensor_tensor(OUT, T, X, ALU.add))
        layernorm(nc, v, act, L, T, A, OUT)
    NodePhase(nc, L, "n3c", [(A, node_rows(L["rank48"][2], 0, D, 0))],
              [(out[0:LAST_P * NB, :].rearrange("(p b) d -> p b d", b=NB), TMP[0:LAST_P, :, :]),
               (out[LAST_P * NB:N, :].rearrange("(p b) d -> p b d", p=1), TMP[LAST_P:LAST_P + 1, 0:LAST_B, :])], compute)


def edge_pass(nc, L, a):
    loc_ns, dst_i, src_f, cut = L["loc_ns"], L["dst_i"], L["src_f"], L["cut"]
    ident, tril, spare, ones_row = L["ident"], L["tril"], L["spare_id"], L["ones_row"]
    WD = D + 1 + GE
    M = D + 2
    AHEAD = 2
    with ExitStack() as c:
        def sb(nm, shape, dt=F32):
            return c.enter_context(nc.sbuf_tensor(f"e_{nm}", shape, dt))

        def ps(nm, shape):
            return c.enter_context(nc.psum_tensor(f"e_{nm}", shape, F32))

        def sem(nm):
            return cleared(nc, c, f"e_{nm}")
        didx = sb("didx", [P, UI, UG], I32)
        sidx = sb("sidx", [P, UI, UG], I32)
        srcs = sb("srcs", [P, 2, UG])
        rows = sb("rows", [P, UI, UG, WD])
        attr = sb("attr", [P, UI, UG, R])
        es = sb("es", [P, UI, UG, GE])
        atT = sb("atT", [R, UG * P])
        hid = sb("hid", [D, UG * P])
        eq = sb("eq", [P, UG, P])
        eqm = sb("eqm", [P, UG, P])
        dup = sb("dup", [P, UG])
        lg = sb("lg", [P, UG])
        tg = sb("tg", [P, UG, GE])
        gt = sb("gt", [P, UG, D])
        msg = sb("msg", [P, UG, M])
        sums = sb("sums", [P, UI, UG, M])
        p_at = ps("p_at", [R, UG * P])
        p_h = ps("p_h", [D, UG * P])
        p_g = [ps(f"p_g{i}", [P, UG, D]) for i in range(2)]
        p_s = [ps(f"p_s{i}", [P, UG, P]) for i in range(2)]
        p_m = ps("p_m", [P, UG, M])
        s_init = sem("attr_cleared")
        s_attr = [sem(f"attr_landed{i}") for i in range(UI)]
        s_didx = sem("dst_staged")
        s_srcs = sem("src_staged")
        s_rows = [sem(f"rows_landed{i}") for i in range(UI)]
        s_at = sem("attr_turned")
        s_atc = sem("attr_copied")
        s_h = sem("hidden_summed")
        s_hid = sem("hidden_done")
        s_g = sem("gate_summed")
        s_s = sem("src_spread")
        s_d = sem("dve_steps")
        s_m = sem("sources_merged")
        s_sum = sem("sums_copied")
        s_put = [sem(f"sums_added{i}") for i in range(UG)]
        clear_all(nc)
        block = c.enter_context(nc.Block())
        LASTG = E // (P * UG)
        LF = (E - LASTG * P * UG) // P
        DS = 12

        @block.sync
        def _(sp):
            at_v = a["edge_attr_40"][0:LASTG * UG * P, :].rearrange("(g j p) d -> p g j d", j=UG, p=P)
            es_v = L["emb_edge"].rearrange("(g j p) d -> p g j d", j=UG, p=P)
            sp.wait_ge(s_init, 1)

            def step(it, first, last):
                for s in range(UI):
                    if not first:
                        sp.wait_ge(s_at, it * UI + (s - UI + 1))
                        nc.sync.nop(nofuse=True)
                        sp.wait_ge(s_d, (it * UI + (s - UI + 1)) * DS)
                    nc.sync.nop(nofuse=True)
                    g = it * UI + s
                    if not last or g < LASTG:
                        sp.dma_start(attr[:, s, :, :], at_v[:, bass.ds(g, 1), :, :].rearrange("p g j d -> p (g j) d")
                                     ).then_inc(s_attr[s], 32)
                    elif g == LASTG:
                        lo = LASTG * UG * P
                        sp.dma_start(attr[:, s, 0:LF, :],
                                     a["edge_attr_40"][lo:lo + LF * P, :].rearrange("(j p) d -> p j d", p=P)
                                     ).then_inc(s_attr[s], 16)
                        sp.dma_start(attr[0:REST, s, LF, :], a["edge_attr_40"][lo + LF * P:E, :]).then_inc(s_attr[s], 16)
                    else:
                        sp.dma_start(attr[:, s, :, :], at_v[:, 0, :, :]).then_inc(s_attr[s], 32)
                    sp.dma_start(es[:, s, :, :], es_v[:, bass.ds(g, 1), :, :].rearrange("p g j d -> p (g j) d")
                                 ).then_inc(s_attr[s], 16)
            run_steps(nc.sync, step)

        @block.gpsimd
        def _(pool):
            def gather(it, s):
                pool.wait_ge(s_didx, it * UI + (s + 1))
                if not (isinstance(it, int) and it == 0):
                    pool.wait_ge(s_d, (it * UI + (s - UI + 1)) * DS)
                nc.gpsimd.nop(nofuse=True)
                for j in range(UG):
                    nc.gpsimd.indirect_dma_start(
                        out=rows[:, s, j, :], out_offset=None, in_=L["tab_dst"][:, :],
                        in_offset=bass.IndirectOffsetOnAxis(ap=didx[:, s, j:j + 1], axis=0)).then_inc(s_rows[s], 16)

            for s in range(AHEAD):
                gather(0, s)

            def step(it, first, last):
                for s in range(UI):
                    if s < UI - AHEAD:
                        gather(it, s + AHEAD)
                    elif not last:
                        gather(it + 1, s + AHEAD - UI)
                    pool.wait_ge(s_sum, it * UI + (s + 1))
                    for j in range(UG):
                        if not (first and s == 0):
                            pool.wait_ge(s_put[j], (it * UI + s) * 16)
                        nc.gpsimd.nop(nofuse=True)
                        nc.gpsimd.indirect_dma_start(
                            out=L["scat"][j][:, :], out_offset=bass.IndirectOffsetOnAxis(ap=sidx[:, s, j:j + 1], axis=0),
                            in_=sums[:, s, j, :], in_offset=None, compute_op=ALU.add).then_inc(s_put[j], 16)
            run_steps(nc.gpsimd, step)
            for j in range(UG):
                pool.wait_ge(s_put[j], 16 * GROUPS)
                pool.wait_ge(s_rows[j], 16 * UG * STEPS)

        @block.scalar
        def _(act):
            def stage(it, s):
                nc.scalar.copy(didx[:, s, :], dst_i[:, bass.ds((it * UI + s) * UG, UG)]).then_inc(s_didx, 1)
            for s in range(UI):
                stage(0, s)

            def front(it, s):
                g1 = it * UI + (s + 1)
                b = s % 2
                if not (isinstance(it, int) and it * UI + s < 2):
                    act.wait_ge(s_d, (it * UI + (s - 1)) * DS)
                nc.scalar.copy(srcs[:, b, :], src_f[:, bass.ds((it * UI + s) * UG, UG)]).then_inc(s_srcs, 1)
                act.wait_ge(s_at, g1)
                nc.scalar.copy(atT[:], p_at[:]).then_inc(s_atc, 1)
                act.wait_ge(s_h, g1)
                nc.scalar.activation(hid[:], p_h[:], ACT.Silu, bias=L["b1c"][:]).then_inc(s_hid, 1)

            front(0, 0)

            def step(it, first, last):
                for s in range(UI):
                    if not (last and s == UI - 1):
                        front(it, s + 1)
                    if not last:
                        act.wait_ge(s_rows[s], it * (16 * UG) + 16 * UG)
                        stage(it + 1, s)
                    act.wait_ge(s_m, it * UI + (s + 1))
                    if not first:
                        for j in range(UG):
                            act.wait_ge(s_put[j], (it * UI + (s - UI + 1)) * 16)
                    nc.scalar.copy(sums[:, s, :, :], p_m[:]).then_inc(s_sum, 1)
            run_steps(nc.scalar, step)

        @block.tensor
        def _(pe):
            def front(it, s):
                g1, sl, b = it * UI + (s + 1), s % UI, s % 2
                w_it = it if s < UI else it + 1
                start = isinstance(it, int) and it * UI + s == 0
                pe.wait_ge(s_attr[sl], w_it * 48 + 48)
                if not start:
                    pe.wait_ge(s_atc, it * UI + s)
                nc.tensor.nop(nofuse=True)
                for j in range(UG):
                    ins = nc.tensor.transpose(p_at[:, j * P:(j + 1) * P], attr[:, sl, j, :], ident[:])
                ins.then_inc(s_at, 1)
                pe.wait_ge(s_srcs, g1)
                if not (isinstance(it, int) and it * UI + s < 2):
                    pe.wait_ge(s_d, (it * UI + (s - 1)) * DS)
                nc.tensor.nop(nofuse=True)
                for j in range(UG):
                    ins = nc.tensor.transpose(p_s[b][:, j, :], srcs[:, b, j:j + 1].to_broadcast([P, P]), ident[:])
                ins.then_inc(s_s, 1)
                pe.wait_ge(s_atc, g1)
                if not start:
                    pe.wait_ge(s_hid, it * UI + s)
                nc.tensor.nop(nofuse=True)
                nc.tensor.matmul(p_h[:], L["w1T"][:], atT[:], start=True, stop=True).then_inc(s_h, 1)
                pe.wait_ge(s_hid, g1)
                nc.tensor.nop(nofuse=True)
                for j in range(UG):
                    nc.tensor.matmul(p_g[b][:, j, :], ones_row[:], L["b2r"][:], start=True, stop=False)
                    ins = nc.tensor.matmul(p_g[b][:, j, :], hid[:, j * P:(j + 1) * P], L["w2T"][:], start=False, stop=True)
                ins.then_inc(s_g, 1)

            front(0, 0)

            def step(it, first, last):
                for s in range(UI):
                    if not (last and s == UI - 1):
                        front(it, s + 1)
                    pe.wait_ge(s_d, (it * UI + (s + 1)) * DS)
                    if not (first and s == 0):
                        pe.wait_ge(s_sum, it * UI + s)
                    nc.tensor.nop(nofuse=True)
                    for j in range(UG):
                        ins = nc.tensor.matmul(p_m[:, j, :], eq[:, j, :], msg[:, j, :], start=True, stop=True)
                    ins.then_inc(s_m, 1)
            run_steps(nc.tensor, step)

        @block.vector
        def _(dve):
            V = nc.vector
            V.memset(attr[:], 0.0).then_inc(s_init, 1)

            def step(it, first, last):
                for s in range(UI):
                    b, n = s % 2, [0]
                    g = it * UI + s

                    def v(ins):
                        n[0] += 1
                        ins.then_inc(s_d, 1)
                        dve.wait_ge(s_d, g * DS + n[0])

                    def c4(t):
                        return t.rearrange("p (g o) -> p g o", o=1)
                    sr = srcs[:, b, :]
                    dve.wait_ge(s_s, it * UI + (s + 1))
                    if not (first and s == 0):
                        dve.wait_ge(s_m, it * UI + s)
                    v(V.tensor_tensor(eq[:], p_s[b][:], c4(sr).to_broadcast([P, UG, P]), ALU.is_equal))
                    v(V.tensor_tensor(eqm[:], eq[:], tril[:].rearrange("p (o q) -> p o q", o=1).to_broadcast([P, UG, P]),
                                      ALU.mult))
                    v(V.tensor_reduce(dup[:], eqm[:], AX.X, ALU.add))
                    v(V.scalar_tensor_tensor(out=dup[:], in0=dup[:], scalar=float(PAD_DST), in1=sr, op0=ALU.mult, op1=ALU.add))
                    if not first:
                        for j in range(UG):
                            dve.wait_ge(s_put[j], (it * UI + (s - UI + 1)) * 16)
                    v(V.tensor_scalar(sidx[:, s, :], dup[:], spare[:], None, ALU.min))
                    dve.wait_ge(s_attr[s], it * 48 + 48)
                    dve.wait_ge(s_rows[s], it * (16 * UG) + 16 * UG)
                    v(V.tensor_tensor(tg[:], es[:, s, :, :], rows[:, s, :, D + 1:WD], ALU.mult))
                    v(V.tensor_reduce(lg[:], tg[:], AX.X, ALU.add))
                    dve.wait_ge(s_g, it * UI + (s + 1))
                    v(V.tensor_tensor(gt[:], p_g[b][:], c4(lg[:]).to_broadcast([P, UG, D]), ALU.add))
                    v(V.tensor_tensor(gt[:], gt[:], c4(cut[:, bass.ds(g * UG, UG)]).to_broadcast([P, UG, D]), ALU.mult))
                    v(V.tensor_copy(msg[:, :, D], rows[:, s, :, D]))
                    v(V.tensor_scalar(msg[:, :, D + 1], loc_ns[:, bass.ds(g * UG, UG)], 0.0, None, ALU.is_ge))
                    v(V.tensor_tensor(msg[:, :, 0:D], gt[:], rows[:, s, :, 0:D], ALU.mult))
                    assert n[0] == DS
            run_steps(nc.vector, step)


_INS = ['x', 'src', 'dst', 'edge_attr_40', 'edge_weight', 'edge_weight1', 'node_type_119', 'node_vec', 'L1_gnn_W1',
        'L1_gnn_b1', 'L1_gnn_W2', 'L1_gnn_b2', 'L1_gnn_emb', 'L1_gnn_adaptW', 'L1_gnn_gamma', 'L1_gnn_beta',
        'L2_gnn_w_rel1', 'L2_gnn_w_root1', 'L2_gnn_b1', 'L2_gnn_w_rel2', 'L2_gnn_w_root2', 'L2_gnn_b2',
        'L3_gnn_weight', 'L3_gnn_bias']


def kernel(**inputs):
    import numpy as _np
    import concourse.bacc as _bacc
    from concourse import mybir as _mybir
    from concourse.bass_utils import run_bass_kernel_spmd as _run

    nc = _bacc.Bacc("TRN2", target_bir_lowering=False, num_devices=1)
    arrays, args = {}, {}
    for name in _INS:
        v = _np.ascontiguousarray(inputs[name])
        arrays[f"in_{name}_dram"] = v
        args[name] = nc.dram_tensor(f"in_{name}_dram", v.shape, _mybir.dt.from_np(v.dtype), kind="ExternalInput").ap()
    out = nc.dram_tensor("out_0_dram", (N, D), _mybir.dt.float32, kind="ExternalOutput").ap()
    gnn(nc, args, out)
    r = _run(nc, [arrays], core_ids=[0])
    return r.results[0]["out_0_dram"]
```

```python
import concourse.bass as bass
from concourse import mybir
from contextlib import ExitStack

F32 = mybir.dt.float32
I32 = mybir.dt.int32
BF16 = mybir.dt.bfloat16
ALU = mybir.AluOpType
ACT = mybir.ActivationFunctionType
AX = mybir.AxisListType

N = 12500
E = 200000
D = 48
R = 40
TYPES = 119
GE = 32
P = 128
NB = -(-N // P)
NP = NB * P
UG = 4
UI = 4
STEPS = -(-E // (P * UG * UI))
GROUPS = STEPS * UI
CHUNKS = GROUPS * UG
KT = -(-CHUNKS // P)
ROWS = KT * P
FULL = E // P
REST = E - FULL * P
PAD_DST = 20000
BIG = 1.5e38
ACC_W = NP + P
EPS = 1e-5
IDX_SPARE = 2 * NP
SCAT_ROWS = NP + P
RB = 7
RSTEPS = NB // (2 * RB)


def bank(nc, c, name, rows, cols):
    return c.enter_context(nc.psum_tensor(name, [P, 512], F32))[0:rows, 0:cols]


def spread_source(nc, L, out, part):
    nc.tensor.matmul(out, part[:, 1:2].to_broadcast([P, P]), L["id_128"][:], start=True, stop=False)
    return nc.tensor.matmul(out, part[:, 2:3].to_broadcast([P, P]), L["id_b"][:], start=False, stop=True)


def run_steps(engine, body):
    body(0, True, False)
    with engine.Fori(1, STEPS - 1) as it:
        body(it, False, False)
    body(STEPS - 1, False, True)


def gnn(nc, a, out):
    ROLES.clear()
    ctx = ExitStack()
    with ctx:
        def dram(name, shape, dt=F32):
            return nc.dram_tensor(name, shape, dt).ap()

        def sb(name, shape, dt=F32, c=ctx):
            return c.enter_context(nc.sbuf_tensor(name, shape, dt))

        tab_in = dram("tab_in", (NP, D + GE))
        tab_dst = dram("tab_dst", (NP, D + 1 + GE))
        tab_rank = dram("tab_rank", (NP + P, D + 1 + GE))
        tab_type = dram("tab_type", (TYPES, 2 * GE))
        tab_h = [dram(f"tab_h{i}", (NP, D)) for i in range(5)]
        emb_edge = dram("emb_edge", (CHUNKS * P, GE))
        rank50 = dram("rank50", (IDX_SPARE, D + 2))
        rank48 = [dram(f"rank48{i}", (IDX_SPARE, D)) for i in range(3)]
        rank96 = dram("rank96", (IDX_SPARE, 2 * D))
        rank144 = dram("rank144", (IDX_SPARE, 3 * D))
        scat = [dram(f"scat{i}", (SCAT_ROWS, D + 2)) for i in range(UG)]

        ident = sb("ident", [P, P])
        iota_row = sb("iota_row", [P, P])
        tril = sb("tril", [P, P])
        ones_row = sb("ones_row", [1, P])
        spare_id = sb("spare_id", [P, 1])
        src_i = sb("src_i", [P, CHUNKS], I32)
        parts = sb("parts", [P, CHUNKS, 3], BF16)
        id_b = sb("id_b", [P, P], BF16)
        id_128 = sb("id_128", [P, P], BF16)
        dup = sb("dup", [P, CHUNKS])
        scat_i = dup[:].bitcast(I32)
        rank_src = sb("rank_src", [P, NB], I32)
        iota_col = sb("iota_col", [P, 1])
        src_f = sb("src_f", [P, CHUNKS])
        loc = sb("loc", [P, CHUNKS + UG])
        loc_ns = sb("loc_ns", [P, CHUNKS + UG])
        exs = sb("exs", [P, CHUNKS + UG, 2])
        cut = sb("cut", [P, CHUNKS])
        win_row = sb("win_row", [1, ROWS], I32)
        node_idx = sb("node_idx", [P, NB], I32)
        dis = sb("dis", [P, NB])
        mult = sb("mult", [P, NB])
        stat = [sb(f"stat{i}", [P, NB]) for i in range(2)]
        X = sb("X", [P, NB, D])
        w1T = sb("w1T", [2 * R, 2 * D])
        b1c = sb("b1c", [2 * D, 1])
        w2T = sb("w2T", [2 * D, 2 * D])
        b2r = sb("b2r", [1, 2 * D])
        gam = sb("gam", [P, D])
        bet = sb("bet", [P, D])
        eps_c = sb("eps_c", [P, 1])
        wrel1 = sb("wrel1", [D, D])
        wrel2 = sb("wrel2", [D, D])
        wroot1 = sb("wroot1", [D, D])
        wroot2 = sb("wroot2", [D, D])
        l2b1 = sb("l2b1", [1, D])
        l2b2 = sb("l2b2", [1, D])
        l3b = sb("l3b", [1, D])
        w3i13 = sb("w3i13", [D, 3 * D])
        w3i2 = sb("w3i2", [D, 2 * D])
        w302 = sb("w302", [D, D])
        id50 = sb("id50", [D + 2, D + 2])

        setup(nc, a, dict(locals()))

        arena = sb("arena", [P, ACC_W])
        OUT = sb("OUT", [P, NB, D])
        tmp_room = sb("tmp_room", [P, NB * (D + 2)])
        TMP = tmp_room[:, 0:NB * D].rearrange("p (b d) -> p b d", d=D)
        L = dict(locals())
        gather_pass(nc, L, "p0", tab_in, D + GE, loc, weights=True, emb_edge=emb_edge)
        rank_nodes(nc, L)
        rank_rows(nc, L, "r0", id50, D + 2, D + 2, rank50)
        nodes0(nc, L)
        rank_table(nc, L)
        edge_pass(nc, L, a)
        nodes1(nc, L)
        gather_pass(nc, L, "p2", tab_h[0], D, loc, dense=(wroot1, l2b1))
        rank_rows(nc, L, "r2", wrel1, D, D, rank48[0])
        nodes2a(nc, L)
        gather_pass(nc, L, "p3", tab_h[1], D, loc, dense=(wroot2, l2b2), dense_in="TMP")
        rank_rows(nc, L, "r3", wrel2, D, D, rank48[1])
        nodes2b(nc, L)
        gather_pass(nc, L, "p4", tab_h[2], D, loc_ns, dense=(w302, l3b))
        rank_rows(nc, L, "r4", w3i13, D, 3 * D, rank144)
        nodes3a(nc, L)
        gather_pass(nc, L, "p5", tab_h[3], D, loc_ns)
        rank_rows(nc, L, "r5", w3i2, D, 2 * D, rank96)
        nodes3b(nc, L)
        gather_pass(nc, L, "p6", tab_h[4], D, loc_ns)
        rank_rows(nc, L, "r6", w3i13[:, 2 * D:3 * D], D, D, rank48[2])
        nodes3c(nc, L, out)


def node_rows(table, lo, hi, width):
    return table[0:NP, :].rearrange("(p b) d -> p b d", b=NB)[:, :, lo:hi]


ZW = NB * D // 4
LAST_P = N // NB
LAST_B = N - LAST_P * NB


def setup(nc, a, L):
    def g(n):
        return L[n]
    ident, X, mult = g("ident"), g("X"), g("mult")
    with ExitStack() as c:
        def sb(name, shape, dt=F32):
            return c.enter_context(nc.sbuf_tensor(name, shape, dt))

        def sem(name):
            return c.enter_context(nc.semaphore(name))
        FW = KT * P
        s_i = sb("s_i", [P, KT, P], I32)
        d_i = sb("d_i", [P, KT, P], I32)
        pl_i = sb("pl_i", [P, KT], I32)
        nf_i = sb("nf_i", [P, KT], I32)
        S = sb("S", [P, KT, P])
        Dd = sb("Dd", [P, KT, P])
        pl = sb("pl", [P, KT])
        nf = sb("nf", [P, KT])
        LG = sb("LG", [P, KT, P])
        DIST = sb("DIST", [P, KT, P])
        V = sb("V", [P, KT, P])
        F = sb("F", [P, KT, P])
        Q = sb("Q", [P, KT, P])
        Mx = s_i[:].bitcast(F32)
        T1 = d_i[:].bitcast(F32)
        PR = sb("PR", [P, KT, P])
        halfpi = sb("halfpi", [P, 1])
        col = [sb(f"col{i}", [P, KT]) for i in range(6)]
        car = sb("car", [P, KT])
        rows = [t[0:1, :, :].rearrange("o k q -> o (k q)") for t in (PR, S, V, DIST)]
        z_i = sb("z_i", [P, NB], I32)
        EP = sb("EP", [P, NB, 2 * GE])
        zero = sb("zero", [P, ZW])
        emb = sb("emb", [TYPES, GE])
        embT = sb("embT", [GE, TYPES])
        adw = sb("adw", [GE, GE])
        adwT = sb("adwT", [GE, GE])
        tt = sb("tt", [TYPES, 2 * GE])
        w1 = sb("w1", [2 * D, 2 * R])
        w2 = sb("w2", [2 * D, 2 * D])
        s_int = sb("s_int", [P, CHUNKS], I32)
        w3 = sb("w3", [D, 4, D])
        ps = [c.enter_context(nc.psum_tensor(f"ps{i}", [P, 4, 512], F32)) for i in range(2)]
        s_ms = sem("s_ms")
        s_ld = sem("s_ld")
        s_nodes = sem("s_nodes")
        s_con = sem("s_con")
        s_v = sem("s_v")
        s_tab = sem("s_tab")
        s_pe = sem("s_pe")
        s_a = sem("s_a")
        s_ep = sem("s_ep")
        s_tt = sem("s_tt")
        s_fin = sem("s_fin")
        s_z = sem("s_z")
        FT = FULL // P
        FR = FULL - FT * P

        block = c.enter_context(nc.Block())
        done, n_sin, n_exp = {}, [0], [0]

        @block.sync
        def _(sp):
            n = [0]

            def ld(dst, src):
                n[0] += 16
                sp.dma_start(dst, src).then_inc(s_ld if "all" in done else s_nodes, 16)

            sp.wait_ge(s_ms, 1)
            for tile, name in ((X, "x"), (mult, "node_vec"), (z_i, "node_type_119")):
                v = a[name]
                if name == "x":
                    ld(tile[0:LAST_P, :, :], v[0:LAST_P * NB, :].rearrange("(p b) d -> p b d", b=NB))
                    ld(tile[LAST_P:LAST_P + 1, 0:LAST_B, :], v[LAST_P * NB:N, :].rearrange("(p b) d -> p b d", p=1))
                else:
                    ld(tile[0:LAST_P, :], v[0:LAST_P * NB].rearrange("(p b) -> p b", b=NB))
                    ld(tile[LAST_P:LAST_P + 1, 0:LAST_B], v[LAST_P * NB:N].rearrange("(p b) -> p b", p=1))
            ld(emb[:], a["L1_gnn_emb"])
            ld(adw[:], a["L1_gnn_adaptW"])
            for h in range(2):
                ld(w1[h * D:(h + 1) * D, h * R:(h + 1) * R], a["L1_gnn_W1"])
                ld(w2[h * D:(h + 1) * D, h * D:(h + 1) * D], a["L1_gnn_W2"])
                ld(g("b1c")[h * D:(h + 1) * D, :], a["L1_gnn_b1"].rearrange("(p o) -> p o", o=1))
                ld(g("b2r")[:, h * D:(h + 1) * D], a["L1_gnn_b2"].rearrange("(p o) -> p o", p=1))
            for t, nm in (("l2b1", "L2_gnn_b1"), ("l2b2", "L2_gnn_b2"), ("l3b", "L3_gnn_bias")):
                ld(g(t)[:], a[nm].rearrange("(p o) -> p o", p=1))
            for t, nm in (("gam", "L1_gnn_gamma"), ("bet", "L1_gnn_beta")):
                ld(g(t)[:], a[nm].rearrange("(p o) -> p o", p=1).to_broadcast([P, D]))
            for t, nm in (("wrel1", "L2_gnn_w_rel1"), ("wrel2", "L2_gnn_w_rel2"), ("wroot1", "L2_gnn_w_root1"),
                          ("wroot2", "L2_gnn_w_root2")):
                ld(g(t)[:], a[nm])
            ld(w3[:], a["L3_gnn_weight"].rearrange("k i o -> i k o"))
            done["all"], n[0] = n[0], 0
            with nc.allow_non_contiguous_dma(reason="one element per chunk"):
                for tile, name in ((s_i, "src"), (d_i, "dst"), (LG, "edge_weight1"), (DIST, "edge_weight")):
                    v = a[name].rearrange("e o -> (e o)") if name == "edge_weight1" else a[name]
                    ld(tile[:, 0:FT, :], v[0:FT * P * P].rearrange("(k q p) -> q k p", q=P, p=P))
                    ld(tile[0:FR, FT, :], v[FT * P * P:FULL * P].rearrange("(q p) -> q p", p=P))
                    ld(tile[FR:FR + 1, FT, 0:REST], v[FULL * P:E].rearrange("(q p) -> q p", q=1))
                before = a["dst"][0:FULL * P].rearrange("(c p) -> c p", p=P)[:, P - 1:P]
                after = a["dst"][0:FULL * P].rearrange("(c p) -> c p", p=P)[:, 0:1]
                ld(pl_i[1:P, 0:1], before[0:P - 1, :])
                ld(pl_i[:, 1:FT], before[P - 1:P * FT - 1, :].rearrange("(k q) o -> q (k o)", q=P))
                ld(pl_i[0:FR + 1, FT:FT + 1], before[P * FT - 1:P * FT + FR, :])
                ld(nf_i[:, 0:FT], after[1:P * FT + 1, :].rearrange("(k q) o -> q (k o)", q=P))
                ld(nf_i[0:FR - 1, FT:FT + 1], after[P * FT + 1:P * FT + FR, :])
                ld(nf_i[FR - 1:FR, FT:FT + 1], a["dst"][FULL * P:FULL * P + 1].rearrange("(q p) -> q p", q=1))
            done["edges"] = n[0]
            sp.wait_ge(s_tt, 1)
            sp.dma_start(g("tab_type")[:, :], tt[:]).then_inc(s_tab, 16)
            z = 0
            for t, w in ((g("rank50"), D + 2), (g("rank48")[0], D), (g("rank48")[1], D), (g("rank48")[2], D),
                         (g("rank96"), 2 * D), (g("rank144"), 3 * D), *((t, D + 2) for t in g("scat"))):
                room = t[0:NP, :].rearrange("(p b) d -> p (b d)", b=NB)
                many = 4 * (w // D)
                sp.dma_start(room[:, 0:many * ZW].rearrange("p (r z) -> p r z", z=ZW),
                             zero[:].rearrange("p (o z) -> p o z", o=1).to_broadcast([P, many, ZW])).then_inc(s_z, 16)
                z += 16
                if w % D:
                    sp.dma_start(room[:, many * ZW:NB * w], zero[:, 0:NB * w - many * ZW]).then_inc(s_z, 16)
                    z += 16
            for t in g("scat"):
                sp.dma_start(t[NP:NP + P, :], zero[:, 0:D + 2]).then_inc(s_z, 16)
                z += 16
            sp.wait_ge(s_nodes, done["all"])
            sp.dma_start(node_rows(g("tab_in"), 0, D, 0), X[:]).then_inc(s_fin, 16)
            sp.wait_ge(s_ep, 16 * NB)
            sp.dma_start(node_rows(g("tab_in"), D, D + GE, 0), EP[:, :, 0:GE]).then_inc(s_fin, 16)
            sp.dma_start(node_rows(g("tab_dst"), D + 1, D + 1 + GE, 0), EP[:, :, GE:2 * GE]).then_inc(s_fin, 16)
            sp.wait_ge(s_fin, 48)
            sp.wait_ge(s_z, z)

        @block.gpsimd
        def _(pool):
            nc.gpsimd.memset(ident[:], 0.0).then_inc(s_con, 1)
            nc.gpsimd.memset(g("tril")[:], 1.0).then_inc(s_con, 1)
            pool.wait_ge(s_con, 2)
            nc.gpsimd.affine_select(out=ident[:], in_=ident[:], compare_op=ALU.not_equal, fill=1.0, base=0,
                                    pattern=[[-1, P]], channel_multiplier=1).then_inc(s_con, 1)
            nc.gpsimd.affine_select(out=g("tril")[:], in_=g("tril")[:], compare_op=ALU.is_gt, fill=0.0, base=0,
                                    pattern=[[-1, P]], channel_multiplier=1).then_inc(s_con, 1)
            nc.gpsimd.iota(g("iota_row")[:], pattern=[[1, P]], base=0, channel_multiplier=0,
                           allow_small_or_imprecise_dtypes=True).then_inc(s_con, 1)
            nc.gpsimd.iota(g("iota_col")[:], pattern=[[1, 1]], base=0, channel_multiplier=1,
                           allow_small_or_imprecise_dtypes=True).then_inc(s_con, 1)
            nc.gpsimd.iota(g("spare_id")[:], pattern=[[1, 1]], base=NP, channel_multiplier=1,
                           allow_small_or_imprecise_dtypes=True).then_inc(s_con, 1)
            pool.wait_ge(s_tab, 16)
            pool.wait_ge(s_nodes, done["all"])
            for b in range(NB):
                nc.gpsimd.indirect_dma_start(
                    out=EP[:, b, :], out_offset=None, in_=g("tab_type")[:, :],
                    in_offset=bass.IndirectOffsetOnAxis(ap=z_i[:, b:b + 1], axis=0)).then_inc(s_ep, 16)
            pool.wait_ge(s_ep, 16 * NB)

        steps = []

        @block.vector
        def _(dve):
            n = [0]

            def v(ins):
                n[0] += 1
                ins.then_inc(s_v, 1)
                dve.wait_ge(s_v, n[0])

            def ask_pe(fn):
                steps.append((n[0], fn))
                dve.wait_ge(s_pe, len(steps))

            V3 = nc.vector
            for t, val in ((s_i, 0), (d_i, PAD_DST), (pl_i, PAD_DST), (nf_i, PAD_DST), (LG, 0.0), (DIST, 0.0),
                           (X, 0.0), (mult, 0.0), (z_i, 0), (g("exs"), 0.0), (w1, 0.0), (w2, 0.0)):
                V3.memset(t[:], val)
            V3.memset(g("loc")[:], -1.0)
            V3.memset(g("loc_ns")[:], -1.0)
            V3.memset(zero[:], 0.0)
            V3.memset(g("ones_row")[:], 1.0)
            V3.memset(halfpi[:], 1.5707963267948966)
            v(V3.memset(g("eps_c")[:], EPS))
            v(V3.memset(PR[:], 1.0))
            V3.memset(PR[:, :, 0:1], 0.0).then_inc(s_ms, 1)
            v(V3.memset(pl_i[0:1, 0:1], -1))
            dve.wait_ge(s_ms, 1)
            dve.wait_ge(s_nodes, done["all"])
            dve.wait_ge(s_con, 7)
            v(V3.memset(col[4][:], 0.0))

            def small(src, dst, m, k):
                buf = ps[0]
                ask_pe(lambda e: nc.tensor.transpose(buf[0:m, 0, 0:k], src, ident[0:k, 0:k]))
                v(V3.tensor_copy(dst, buf[0:m, 0, 0:k]))

            small(emb[:], embT[:], GE, TYPES)
            small(adw[:], adwT[:], GE, GE)
            ask_pe(lambda e: nc.tensor.matmul(ps[0][0:TYPES, 0, 0:GE], embT[:], adwT[:], start=True, stop=True))
            V3.tensor_copy(tt[:, 0:GE], emb[:])
            v(V3.tensor_copy(tt[:, GE:2 * GE], ps[0][0:TYPES, 0, 0:GE]))
            V3.memset(col[5][:], 0.0).then_inc(s_tt, 1)
            small(w1[:], g("w1T")[:], 2 * R, 2 * D)
            small(w2[:], g("w2T")[:], 2 * D, 2 * D)
            V3.tensor_copy(g("id_b")[:], ident[:])
            V3.tensor_scalar(g("id_128")[:], ident[:], float(P), None, ALU.mult)
            V3.tensor_copy(g("id50")[:], ident[0:D + 2, 0:D + 2])
            V3.tensor_copy(g("w3i13")[:, 0:D], ident[0:D, 0:D])
            V3.tensor_copy(g("w3i13")[:, D:2 * D], w3[:, 1, :])
            V3.tensor_copy(g("w3i13")[:, 2 * D:3 * D], w3[:, 3, :])
            V3.tensor_copy(g("w3i2")[:, 0:D], ident[0:D, 0:D])
            V3.tensor_copy(g("w3i2")[:, D:2 * D], w3[:, 2, :])
            v(V3.tensor_tensor(g("w302")[:], w3[:, 0, :], w3[:, 2, :], ALU.subtract))
            dve.wait_ge(s_ld, done["edges"])
            V3.tensor_copy(S[:], s_i[:])
            V3.tensor_copy(pl[:], pl_i[:])
            V3.tensor_copy(nf[:], nf_i[:])
            v(V3.tensor_copy(Dd[:], d_i[:]))
            V3.tensor_tensor(F[:, :, 1:P], Dd[:, :, 1:P], Dd[:, :, 0:P - 1], ALU.not_equal)
            V3.tensor_tensor(F[:, :, 0], Dd[:, :, 0], pl[:], ALU.not_equal)
            v(V3.tensor_scalar(V[:], Dd[:], float(PAD_DST - 1), None, ALU.is_lt))
            v(V3.tensor_tensor_scan(out=T1.rearrange("p k q -> p (k q)"), data0=PR[:].rearrange("p k q -> p (k q)"),
                                    data1=F[:].rearrange("p k q -> p (k q)"), initial=0.0, op0=ALU.mult, op1=ALU.add))
            V3.tensor_copy(col[0][:], T1[:, :, P - 1])
            v(V3.tensor_tensor(Mx, T1, F[:, :, 0:1].to_broadcast([P, KT, P]), ALU.subtract))
            V3.tensor_copy(col[1][:], F[:, :, 0])
            v(V3.scalar_tensor_tensor(out=Q[:].rearrange("p k q -> p (k q)"), in0=Mx.rearrange("p k q -> p (k q)"),
                                      scalar=1.0, in1=V[:].rearrange("p k q -> p (k q)"), op0=ALU.add, op1=ALU.mult))
            v(V3.tensor_scalar(T1, Q[:], -1.0, None, ALU.add))

            def to_cols(src, dst, w=CHUNKS, conv=None):
                buf = ps[0]

                def pe(e):
                    for k in range(KT):
                        ins = nc.tensor.transpose(buf[:, k // 4, (k % 4) * P:(k % 4 + 1) * P], src[:, k, :], ident[:])
                    return ins
                ask_pe(pe)
                v(V3.tensor_copy(dst, buf[:].rearrange("p a b -> p (a b)")[:, 0:w]))

            to_cols(S, g("src_i")[:])
            to_cols(T1, g("loc")[:, 0:CHUNKS])
            v(V3.tensor_tensor(Mx, S[:], Dd[:], ALU.not_equal))
            v(V3.tensor_tensor(Q[:], Q[:], Mx, ALU.mult))
            v(V3.tensor_scalar(Q[:], Q[:], -1.0, None, ALU.add))
            to_cols(Q, g("loc_ns")[:, 0:CHUNKS])
            v(V3.scalar_tensor_tensor(out=Q[:].rearrange("p k q -> p (k q)"), in0=Dd[:].rearrange("p k q -> p (k q)"),
                                      scalar=1.0, in1=V[:].rearrange("p k q -> p (k q)"), op0=ALU.add, op1=ALU.mult))
            v(V3.tensor_tensor(Q[:], Q[:], F[:], ALU.mult))
            to_cols(Q, g("exs")[:, 0:CHUNKS, 1])
            v(V3.tensor_scalar(Q[:], V[:], -float(PAD_DST), float(PAD_DST), ALU.mult, ALU.add))
            v(V3.tensor_tensor(Q[:], Q[:], S[:], ALU.add))
            to_cols(Q, g("src_f")[:])
            parts = g("parts")
            V3.tensor_copy(parts[:, :, 0], g("loc")[:, 0:CHUNKS])
            v(V3.tensor_copy(s_int[:], g("src_f")[:]))
            v(V3.tensor_scalar(s_int[:], s_int[:], 7, None, ALU.arith_shift_right))
            v(V3.tensor_copy(parts[:, :, 1], s_int[:]))
            v(V3.tensor_copy(s_int[:], g("src_f")[:]))
            v(V3.tensor_scalar(s_int[:], s_int[:], P - 1, None, ALU.bitwise_and))
            v(V3.tensor_copy(parts[:, :, 2], s_int[:]))
            v(V3.tensor_scalar(DIST[:], DIST[:], 6.0, None, ALU.min))
            n_sin[0] = n[0]
            dve.wait_ge(s_a, 1)
            v(V3.tensor_tensor(DIST[:], DIST[:], DIST[:], ALU.mult))
            to_cols(DIST, g("cut")[:])

            def to_row(src, dst):
                buf = ps[1]

                def pe(e):
                    for k in range(KT):
                        ins = nc.tensor.matmul(buf[0:1, k // 4, (k % 4) * P:(k % 4 + 1) * P], src[:, k:k + 1], ident[:],
                                               start=True, stop=True)
                    return ins
                ask_pe(pe)
                v(V3.tensor_copy(dst, buf[0:1, :, :].rearrange("p a b -> p (a b)")[:, 0:ROWS]))

            def from_row(src, dst):
                buf = ps[1]

                def pe(e):
                    for k in range(KT):
                        ins = nc.tensor.matmul(buf[:, 0, k:k + 1], src[0:1, k * P:(k + 1) * P], g("ones_row")[0:1, 0:1],
                                               start=True, stop=True)
                    return ins
                ask_pe(pe)
                v(V3.tensor_copy(dst[:], buf[:, 0, 0:KT]))

            to_row(col[0], rows[0])
            to_row(col[1], rows[1])
            v(V3.memset(rows[3], 0.0))
            v(V3.tensor_tensor_scan(out=rows[2], data0=rows[3], data1=rows[0], initial=0.0, op0=ALU.add, op1=ALU.add))
            v(V3.tensor_tensor(rows[2], rows[2], rows[0], ALU.subtract))
            v(V3.tensor_tensor(rows[2], rows[2], rows[1], ALU.add))
            v(V3.tensor_scalar(g("win_row")[:], rows[2], -1.0, None, ALU.add))

            flat = lambda t: t[:, :, :].rearrange("p k q -> p (k q)")
            ends = T1
            V3.tensor_copy(ends[:, :, 0:P - 1], F[:, :, 1:P])
            v(V3.tensor_tensor(ends[:, :, P - 1], Dd[:, :, P - 1], nf[:], ALU.not_equal))
            v(V3.tensor_reduce(col[0][:], F[:], AX.X, ALU.max))
            v(V3.tensor_reduce(col[1][:], ends[:], AX.X, ALU.max))
            for t in (F, ends, col[0], col[1]):
                w = t if t is T1 else t[:]
                v(V3.tensor_scalar(w, w, -2.0 * BIG, BIG, ALU.mult, ALU.add))
            for rev, guard, hs, edge, tail, vals in ((False, F, col[0], 0, P - 1, LG), (True, ends, col[1], P - 1, 0, Mx)):
                fl = (lambda x: x[:, ::-1]) if rev else (lambda x: x)
                v(V3.tensor_copy(col[2][:], guard[:, :, edge]))
                v(V3.memset(guard[:, :, edge:edge + 1], -BIG))
                if not rev:
                    v(V3.tensor_copy(Q[:], LG[:]))
                    src_t = Q
                else:
                    src_t = Q
                v(V3.tensor_tensor_scan(out=fl(flat(Mx)), data0=fl(flat(guard)), data1=fl(flat(src_t)), initial=-BIG,
                                        op0=ALU.min, op1=ALU.max))
                v(V3.tensor_copy(col[3][:], Mx[:, :, tail]))
                to_row(col[3], rows[0])
                to_row(hs, rows[1])
                v(V3.tensor_tensor_scan(out=fl(rows[2]), data0=fl(rows[1]), data1=fl(rows[0]), initial=-BIG,
                                        op0=ALU.min, op1=ALU.max))
                v(V3.memset(rows[3], -BIG))
                if rev:
                    v(V3.tensor_copy(rows[3][:, 0:ROWS - 1], rows[2][:, 1:ROWS]))
                else:
                    v(V3.tensor_copy(rows[3][:, 1:ROWS], rows[2][:, 0:ROWS - 1]))
                from_row(rows[3], car)
                v(V3.tensor_tensor(car[:], car[:], col[2][:], ALU.min))
                v(V3.tensor_tensor(src_t[:, :, edge], src_t[:, :, edge], car[:], ALU.max))
                v(V3.tensor_tensor_scan(out=fl(flat(Mx)), data0=fl(flat(guard)), data1=fl(flat(src_t)), initial=-BIG,
                                        op0=ALU.min, op1=ALU.max))
                if not rev:
                    v(V3.tensor_copy(Q[:], Mx))
            v(V3.tensor_tensor(LG[:], LG[:], Mx, ALU.subtract))
            n_exp[0] = n[0]
            dve.wait_ge(s_a, 2)
            v(V3.tensor_copy(LG[:], LG[:]))
            to_cols(LG, g("exs")[:, 0:CHUNKS, 0])

        @block.scalar
        def _(act):
            act.wait_ge(s_v, n_sin[0])
            nc.scalar.activation(DIST[:], DIST[:], ACT.Sin, bias=halfpi[:], scale=-3.141592653589793 / 12).then_inc(s_a, 1)
            act.wait_ge(s_v, n_exp[0])
            nc.scalar.activation(LG[:], LG[:], ACT.Exp).then_inc(s_a, 1)

        @block.tensor
        def _(pe):
            pe.wait_ge(s_con, 7)
            for n_v, fn in steps:
                pe.wait_ge(s_v, n_v)
                fn(pe).then_inc(s_pe, 1)


def cleared(nc, c, role):
    if role not in ROLES:
        ROLES[role] = nc.alloc_semaphore(role)
    else:
        CLEAR.append(ROLES[role])
    return ROLES[role]


ROLES = {}
CLEAR = []


def clear_all(nc):
    if not CLEAR:
        return
    with nc.Block() as block:
        @block.gpsimd
        def _(pool):
            low, high = min(s.num for s in CLEAR), max(s.num for s in CLEAR) + 1
            nc.gpsimd.dma_reset(range(low, high))
            for s in CLEAR:
                nc.gpsimd.sem_clear(s)
    CLEAR.clear()


def gather_pass(nc, L, name, table, width, loc, weights=False, emb_edge=None, dense=None, dense_in="X"):
    arena, iota_row, X, OUT = L["arena"], L["iota_row"], L["X"], L["OUT"]
    DI = L[dense_in]
    exs, src_i, win_row, ident, ones_row = L["exs"], L["src_i"], L["win_row"], L["ident"], L["ones_row"]
    M = D + 2 if weights else D
    with ExitStack() as c:
        def sb(nm, shape, dt=F32):
            return c.enter_context(nc.sbuf_tensor(f"{name}_{nm}", shape, dt))

        def sem(nm):
            return cleared(nc, c, f"pass_{nm}")
        idx = sb("idx", [P, UI, UG], I32)
        rows = sb("rows", [P, UI, UG, width])
        hot = sb("hot", [P, 2, UG, P])
        msg = sb("msg", [P, 2, UG, M]) if weights else None
        xs = sb("xs", [P, D])
        xT = sb("xT", [D, P])
        win = c.enter_context(nc.psum_tensor(f"{name}_win", [D + 2, 2, UG, P], F32))
        dt_ps = bank(nc, c, f"{name}_dt", D, P)
        do_ps = bank(nc, c, f"{name}_do", P, D)
        s_idx = sem("idx_staged")
        s_rows = [sem(f"rows_landed{i}") for i in range(UI)]
        s_hot = sem("onehot_built")
        s_msg = sem("messages_built")
        s_win = sem("window_summed")
        s_acc = sem("window_added")
        if weights:
            srcs = sb("srcs", [P, 2, UG])
            part = sb("part", [P, 2, UG, 3], BF16)
            dups = sb("dups", [P, 2, UG])
            junk = sb("junk", [P, UG, P])
            spread = [c.enter_context(nc.psum_tensor(f"{name}_spread{i}", [P, UG, P], F32)) for i in range(2)]
        s_srcs = sem("sources_staged") if weights else None
        s_spr = sem("sources_spread") if weights else None
        s_dup = sem("duplicates_counted") if weights else None
        s_dupc = sem("duplicates_copied") if weights else None
        s_emb = [sem(f"embeddings_stored{i}") for i in range(UI)] if weights else None
        s_xs = sem("block_staged")
        s_dt = sem("block_turned")
        s_xT = sem("turned_copied")
        s_do = sem("block_multiplied")
        s_out = sem("block_out")
        clear_all(nc)
        block = c.enter_context(nc.Block())

        @block.gpsimd
        def _(pool):
            def step(it, first, last):
                for s in range(UI):
                    pool.wait_ge(s_idx, it * UI + (s + 1))
                    if not first:
                        if weights:
                            pool.wait_ge(s_msg, it * UI + (s - UI + 1))
                            pool.wait_ge(s_emb[s], it * 16)
                        else:
                            pool.wait_ge(s_win, it * UI + (s - UI + 1))
                    nc.gpsimd.nop(nofuse=True)
                    for j in range(UG):
                        nc.gpsimd.indirect_dma_start(
                            out=rows[:, s, j, :], out_offset=None, in_=table[:, :],
                            in_offset=bass.IndirectOffsetOnAxis(ap=idx[:, s, j:j + 1], axis=0)).then_inc(s_rows[s], 16)
            run_steps(nc.gpsimd, step)
            for s in range(UI):
                pool.wait_ge(s_rows[s], 16 * UG * STEPS)

        if weights:
            @block.sync
            def _(sp):
                store = emb_edge.rearrange("(g j p) d -> p g j d", j=UG, p=P)

                def step(it, first, last):
                    for s in range(UI):
                        sp.wait_ge(s_rows[s], it * (16 * UG) + 16 * UG)
                        nc.sync.nop(nofuse=True)
                        sp.dma_start(store[:, bass.ds(it * UI + s, 1), :, :].rearrange("p g j d -> p (g j) d"),
                                     rows[:, s, :, D:D + GE]).then_inc(s_emb[s], 16)
                run_steps(nc.sync, step)
                for s in range(UI):
                    sp.wait_ge(s_emb[s], 16 * STEPS)

        @block.scalar
        def _(act):
            def stage(it, s):
                nc.scalar.copy(idx[:, s, :], src_i[:, bass.ds((it * UI + s) * UG, UG)]).then_inc(s_idx, 1)

            def sources(it, s):
                if not (isinstance(it, int) and it * UI + s < 2):
                    act.wait_ge(s_dup, (it * UI + (s - 1)) * UG)
                nc.scalar.copy(part[:, s % 2, :, :], L["parts"][:, bass.ds((it * UI + s) * UG, UG), :])
                nc.scalar.copy(srcs[:, s % 2, :], L["src_f"][:, bass.ds((it * UI + s) * UG, UG)]).then_inc(s_srcs, 1)

            for s in range(UI):
                stage(0, s)
            if weights:
                sources(0, 0)

            def step(it, first, last):
                if dense:
                    if not first:
                        act.wait_ge(s_dt, it)
                    nc.scalar.copy(xs[:], DI[:, bass.ds(it, 1), :].rearrange("p o d -> p (o d)")).then_inc(s_xs, 1)
                for s in range(UI):
                    if not last:
                        act.wait_ge(s_rows[s], it * (16 * UG) + 16 * UG)
                        stage(it + 1, s)
                    if weights:
                        if not (last and s == UI - 1):
                            sources(it, s + 1)
                        act.wait_ge(s_dup, (it * UI + (s + 1)) * UG)
                        nc.scalar.copy(L["dup"][:, bass.ds((it * UI + s) * UG, UG)], dups[:, s % 2, :]).then_inc(s_dupc, 1)
                    if dense and s == 1:
                        act.wait_ge(s_dt, it + 1)
                        if not first:
                            act.wait_ge(s_do, it)
                        nc.scalar.copy(xT[:], dt_ps).then_inc(s_xT, 1)
                    if dense and s == 3:
                        act.wait_ge(s_do, it + 1)
                        nc.scalar.copy(OUT[:, bass.ds(it, 1), :].rearrange("p o d -> p (o d)"),
                                       do_ps).then_inc(s_out, 1)
            run_steps(nc.scalar, step)

        @block.vector
        def _(dve):
            nc.vector.memset(arena[0:M, :], 0.0).then_inc(s_acc, 1)
            dve.wait_ge(s_acc, 1)

            def build(it, s):
                nx, b = s % UI, s % 2
                if not (isinstance(it, int) and it * UI + s < 2):
                    dve.wait_ge(s_win, it * UI + (s - 1))
                nc.vector.tensor_tensor(
                    hot[:, b, :, :], iota_row[:].rearrange("p (o q) -> p o q", o=1).to_broadcast([P, UG, P]),
                    loc[:, bass.ds((it * UI + s) * UG, UG)].rearrange("p (g o) -> p g o", o=1).to_broadcast([P, UG, P]),
                    ALU.is_equal).then_inc(s_hot, 1)
                if weights:
                    e = exs[:, bass.ds((it * UI + s) * UG, UG), :]
                    wait_it = it if s < UI else it + 1
                    dve.wait_ge(s_rows[nx], wait_it * (16 * UG) + 16 * UG)
                    nc.vector.tensor_copy(msg[:, b, :, D:D + 2], e)
                    nc.vector.tensor_tensor(msg[:, b, :, 0:D], rows[:, nx, :, 0:D],
                                            e[:, :, 0:1].to_broadcast([P, UG, D]), ALU.mult).then_inc(s_msg, 1)

            def count(it, s):
                b = s % 2
                dve.wait_ge(s_spr, it * UI + (s + 1))
                if not (isinstance(it, int) and it * UI + s < 2):
                    dve.wait_ge(s_dupc, it * UI + (s - 1))
                for j in range(UG):
                    nc.vector.scalar_tensor_tensor(out=junk[:, j, :], in0=spread[b][:, j, :], scalar=srcs[:, b, j:j + 1],
                                                   in1=L["tril"][:], op0=ALU.is_equal, op1=ALU.mult,
                                                   accum_out=dups[:, b, j:j + 1]).then_inc(s_dup, 1)

            build(0, 0)

            def step(it, first, last):
                for s in range(UI):
                    if not (last and s == UI - 1):
                        build(it, s + 1)
                    if weights:
                        if not (first and s == 0):
                            dve.wait_ge(s_dup, (it * UI + s) * UG)
                        count(it, s)
                    _, at = nc.values_load_multi_w_load_instructions(
                        win_row[0:1, bass.ds((it * UI + s) * UG, UG)], engines=[mybir.EngineType.DVE],
                        min_val=0, max_val=NP)
                    dve.wait_ge(s_win, it * UI + (s + 1))
                    for j in range(UG):
                        into = arena[0:M, bass.ds(at[j], P)]
                        nc.vector.tensor_tensor(into, into, win[0:M, s % 2, j, :], ALU.add).then_inc(s_acc, 1)
                        dve.wait_ge(s_acc, (it * UI + s) * UG + (j + 2))
            run_steps(nc.vector, step)

        @block.tensor
        def _(pe):
            def step(it, first, last):
                for s in range(UI):
                    b = s % 2
                    if weights:
                        pe.wait_ge(s_srcs, it * UI + (s + 1))
                        if not (first and s < 2):
                            pe.wait_ge(s_dup, (it * UI + (s - 1)) * UG)
                        nc.tensor.nop(nofuse=True)
                        for j in range(UG):
                            ins = spread_source(nc, L, spread[b][:, j, :], part[:, b, j, :])
                        ins.then_inc(s_spr, 1)
                    pe.wait_ge(s_hot, it * UI + (s + 1))
                    if weights:
                        pe.wait_ge(s_msg, it * UI + (s + 1))
                    else:
                        pe.wait_ge(s_rows[s], it * (16 * UG) + 16 * UG)
                    if not (first and s < 2):
                        pe.wait_ge(s_acc, (it * UI + s - 1) * UG + 1)
                    nc.tensor.nop(nofuse=True)
                    for j in range(UG):
                        ins = nc.tensor.matmul(win[0:M, b, j, :], msg[:, b, j, :] if weights else rows[:, s, j, :],
                                               hot[:, b, j, :], start=True, stop=True)
                    ins.then_inc(s_win, 1)
                    if dense and s == 1:
                        pe.wait_ge(s_xs, it + 1)
                        if not first:
                            pe.wait_ge(s_xT, it)
                        nc.tensor.nop(nofuse=True)
                        nc.tensor.transpose(dt_ps, xs[:], ident[:]).then_inc(s_dt, 1)
                    if dense and s == 3:
                        pe.wait_ge(s_xT, it + 1)
                        if not first:
                            pe.wait_ge(s_out, it)
                        nc.tensor.nop(nofuse=True)
                        nc.tensor.matmul(do_ps, ones_row[:], dense[1][:], start=True, stop=False)
                        nc.tensor.matmul(do_ps, xT[:], dense[0][:], start=False, stop=True).then_inc(s_do, 1)
            run_steps(nc.tensor, step)


def rank_nodes(nc, L):
    arena, id50, node_idx, stat = L["arena"], L["id50"], L["node_idx"], L["stat"]
    with ExitStack() as c:
        nd = bank(nc, c, "rn_ps", P, NB)
        rid = c.enter_context(nc.sbuf_tensor("rn_id", [P, NB], F32))
        s_pe = cleared(nc, c, "rn_turned")
        s_v = cleared(nc, c, "rn_dve")
        s_io = cleared(nc, c, "rn_iota")
        clear_all(nc)
        block = c.enter_context(nc.Block())

        @block.gpsimd
        def _(pool):
            nc.gpsimd.iota(rid[:], pattern=[[P, NB]], base=NP + 1, channel_multiplier=1,
                           allow_small_or_imprecise_dtypes=True).then_inc(s_io, 1)

        @block.tensor
        def _(pe):
            for b in range(NB):
                ins = nc.tensor.matmul(nd[:, b:b + 1], arena[0:D + 2, b * P:(b + 1) * P], id50[:, D + 1:D + 2],
                                       start=True, stop=True)
            ins.then_inc(s_pe, 1)

        @block.vector
        def _(dve):
            dve.wait_ge(s_pe, 1)
            dve.wait_ge(s_io, 1)
            nc.vector.tensor_scalar(stat[0][:], nd, 0.5, None, ALU.is_lt).then_inc(s_v, 1)
            dve.wait_ge(s_v, 1)
            nc.vector.tensor_tensor(stat[0][:], stat[0][:], rid[:], ALU.mult).then_inc(s_v, 1)
            dve.wait_ge(s_v, 2)
            nc.vector.scalar_tensor_tensor(out=node_idx[:], in0=nd, scalar=-1.0, in1=stat[0][:],
                                           op0=ALU.add, op1=ALU.add).then_inc(s_v, 1)
            dve.wait_ge(s_v, 3)
            nc.vector.tensor_scalar(L["rank_src"][:], node_idx[:], float(N - 1), None, ALU.min)
            nc.vector.scalar_tensor_tensor(out=L["dup"][:], in0=L["dup"][:], scalar=float(PAD_DST), in1=L["src_f"][:],
                                           op0=ALU.mult, op1=ALU.add).then_inc(s_v, 1)
            dve.wait_ge(s_v, 4)
            nc.vector.tensor_scalar(L["scat_i"], L["dup"][:], L["spare_id"][:], None, ALU.min).then_inc(s_v, 1)


def rank_table(nc, L):
    W = D + 1 + GE
    rows = L["arena"][:, 0:NB * W].rearrange("p (b d) -> p b d", d=W)
    with ExitStack() as c:
        s_g = cleared(nc, c, "rt_gathered")
        s_st = cleared(nc, c, "rt_stored")
        clear_all(nc)
        block = c.enter_context(nc.Block())

        @block.gpsimd
        def _(pool):
            for b in range(NB):
                nc.gpsimd.indirect_dma_start(
                    out=rows[:, b, :], out_offset=None, in_=L["tab_dst"][:, :],
                    in_offset=bass.IndirectOffsetOnAxis(ap=L["rank_src"][:, b:b + 1], axis=0)).then_inc(s_g, 16)
            pool.wait_ge(s_g, 16 * NB)

        @block.sync
        def _(sp):
            sp.wait_ge(s_g, 16 * NB)
            sp.dma_start(L["tab_rank"][0:NP, :].rearrange("(b p) d -> p b d", p=P), rows[:]).then_inc(s_st, 16)
            sp.dma_start(L["tab_rank"][NP:NP + P, :], rows[:, 0, :]).then_inc(s_st, 16)
            sp.wait_ge(s_st, 32)


def rank_rows(nc, L, name, mat, K, W, table):
    arena, node_idx = L["arena"], L["node_idx"]
    with ExitStack() as c:
        def sb(nm, shape, dt=F32):
            return c.enter_context(nc.sbuf_tensor(f"{name}_{nm}", shape, dt))

        def sem(nm):
            return cleared(nc, c, f"ranks_{nm}")
        blk = sb("blk", [D + 2, 2, RB, P])
        idx = sb("idx", [P, 2, RB], I32)
        rows = sb("rows", [P, 2, RB, W])
        ps = [c.enter_context(nc.psum_tensor(f"{name}_ps{i}", [P, RB + 1, 256], F32)) for i in range(2)]
        s_blk = sem("blocks_staged")
        s_idx = sem("idx_staged")
        s_ps = sem("blocks_multiplied")
        s_rows = sem("rows_copied")
        s_put = [sem(f"rows_stored{i}") for i in range(2)]
        clear_all(nc)
        block = c.enter_context(nc.Block())

        def steps(engine, body):
            body(0, True)
            with engine.Fori(1, RSTEPS) as it:
                body(it, False)

        @block.scalar
        def _(act):
            def step(it, first):
                for s in range(2):
                    if not first:
                        act.wait_ge(s_ps, it * 2 + (s - 1))
                        act.wait_ge(s_put[s], it * (16 * RB))
                    nc.scalar.copy(blk[0:K, s, :, :].rearrange("k r p -> k (r p)"),
                                   arena[0:K, bass.ds((it * 2 + s) * (RB * P), RB * P)]).then_inc(s_blk, 1)
                    nc.scalar.copy(idx[:, s, :], node_idx[:, bass.ds((it * 2 + s) * RB, RB)]).then_inc(s_idx, 1)
            steps(nc.scalar, step)

        @block.tensor
        def _(pe):
            def step(it, first):
                for s in range(2):
                    pe.wait_ge(s_blk, it * 2 + (s + 1))
                    if not first:
                        pe.wait_ge(s_rows, it * 2 + (s - 1))
                    nc.tensor.nop(nofuse=True)
                    for r in range(RB):
                        ins = nc.tensor.matmul(ps[s][:, r, 0:W], blk[0:K, s, r, :], mat[0:K, 0:W], start=True, stop=True)
                    ins.then_inc(s_ps, 1)
            steps(nc.tensor, step)

        @block.vector
        def _(dve):
            def step(it, first):
                for s in range(2):
                    dve.wait_ge(s_ps, it * 2 + (s + 1))
                    if not first:
                        dve.wait_ge(s_put[s], it * (16 * RB))
                    nc.vector.tensor_copy(rows[:, s, :, :], ps[s][:, 0:RB, 0:W]).then_inc(s_rows, 1)
            steps(nc.vector, step)

        @block.gpsimd
        def _(pool):
            def step(it, first):
                for s in range(2):
                    pool.wait_ge(s_rows, it * 2 + (s + 1))
                    pool.wait_ge(s_idx, it * 2 + (s + 1))
                    nc.gpsimd.nop(nofuse=True)
                    for r in range(RB):
                        nc.gpsimd.indirect_dma_start(
                            out=table[:, :], out_offset=bass.IndirectOffsetOnAxis(ap=idx[:, s, r:r + 1], axis=0),
                            in_=rows[:, s, r, :], in_offset=None).then_inc(s_put[s], 16)
            steps(nc.gpsimd, step)
            for s in range(2):
                pool.wait_ge(s_put[s], 16 * RB * RSTEPS)


class NodePhase:

    def __init__(self, nc, L, name, loads, stores, compute, halves=False):
        with ExitStack() as c:
            s_ld = [cleared(nc, c, f"nodes_loaded{i}") for i in range(len(loads))]
            s_v = cleared(nc, c, "nodes_dve")
            s_a = cleared(nc, c, "nodes_act")
            s_st = cleared(nc, c, "nodes_stored")
            clear_all(nc)
            block = c.enter_context(nc.Block())
            asks, ready = [], {}

            @block.vector
            def _(dve):
                n = [0]

                def v(ins):
                    n[0] += 1
                    ins.then_inc(s_v, 1)
                    dve.wait_ge(s_v, n[0])

                def act(fn):
                    asks.append((n[0], fn))
                    dve.wait_ge(s_a, len(asks))

                def loaded(i):
                    dve.wait_ge(s_ld[i], 16)

                def free(i):
                    ready[i] = n[0]
                if halves:
                    for h in range(2):
                        loaded(h)
                        compute(nc, v, act, half(h))
                        ready["store", h] = n[0]
                else:
                    compute(nc, v, act, loaded, free)
                ready["end"] = n[0]

            @block.scalar
            def _(act):
                for at, fn in asks:
                    act.wait_ge(s_v, at)
                    fn().then_inc(s_a, 1)

            @block.sync
            def _(sp):
                for i, (dst, src) in enumerate(loads):
                    if i in ready:
                        sp.wait_ge(s_v, ready[i])
                    sp.dma_start(dst, src).then_inc(s_ld[i], 16)
                for i, (dst, src) in enumerate(stores):
                    sp.wait_ge(s_v, ready.get(("store", i), ready["end"]))
                    sp.dma_start(dst, src).then_inc(s_st, 16)
                sp.wait_ge(s_st, 16 * len(stores))


def half(h):
    return slice(h * (NB // 2), (h + 1) * (NB // 2))


def bc(t):
    return t.rearrange("p (b o) -> p b o", o=1).to_broadcast([P, t.shape[1], D])


def in_halves(dst, src):
    return [(dst[:, half(h), :], src[:, half(h), :]) for h in range(2)]


def layernorm(nc, v, act, L, dst, tmp, src, part=slice(0, NB)):
    m, r = L["stat"][0][:, part], L["stat"][1][:, part]
    V = nc.vector
    v(V.tensor_reduce(m, src, AX.X, ALU.add))
    v(V.tensor_scalar(m, m, 1.0 / D, None, ALU.mult))
    v(V.tensor_tensor(dst, src, bc(m), ALU.subtract))
    v(V.tensor_tensor(tmp, dst, dst, ALU.mult))
    v(V.tensor_reduce(r, tmp, AX.X, ALU.add))
    act(lambda: nc.scalar.activation(r, r, ACT.Sqrt, bias=L["eps_c"][:], scale=1.0 / D))
    v(V.reciprocal(r, r))
    v(V.tensor_tensor(dst, dst, bc(r), ALU.mult))


def room(L, at, width, blocks=NB):
    return L["arena"][:, at:at + blocks * width].rearrange("p (b d) -> p b d", d=width)


def nodes0(nc, L):
    A, X, TMP, OUT, st = room(L, 0, D + 2), L["X"][:], L["TMP"], L["OUT"][:], L["stat"]

    def compute(nc, v, act, loaded, free):
        V = nc.vector
        loaded(0)
        v(V.tensor_scalar(st[0][:], A[:, :, D], 0.5, None, ALU.max))
        v(V.reciprocal(st[0][:], st[0][:]))
        v(V.tensor_tensor(TMP, A[:, :, 0:D], bc(st[0][:]), ALU.mult))
        v(V.tensor_scalar(OUT, TMP, 0.0, None, ALU.min))
        act(lambda: nc.scalar.activation(OUT, OUT, ACT.Exp))
        v(V.tensor_scalar(TMP, TMP, 0.0, -1.0, ALU.max, ALU.add))
        v(V.tensor_tensor(TMP, TMP, OUT, ALU.add))
        v(V.tensor_tensor(TMP, TMP, X, ALU.add))
        layernorm(nc, v, act, L, X, OUT, TMP)
        v(V.tensor_tensor(TMP, X, bc(L["mult"][:]), ALU.mult))
    with nc.allow_non_contiguous_dma(reason="one column of the table"):
        NodePhase(nc, L, "n0", [(A, node_rows(L["rank50"], 0, D + 2, 0))],
                  [(node_rows(L["tab_dst"], 0, D, 0), TMP),
                   (node_rows(L["tab_dst"], D, D + 1, 0), L["mult"][:].rearrange("p (b o) -> p b o", o=1))], compute)


def nodes1(nc, L):
    W = D + 2
    A, X, TMP, OUT, st = room(L, 0, W), L["X"][:], L["TMP"], L["OUT"][:], L["stat"]
    B = [room(L, NB * W, W), L["tmp_room"][:].rearrange("p (b d) -> p b d", d=W)]
    dis = L["dis"][:]

    def rows(i):
        return L["scat"][i][0:NP, :].rearrange("(p b) d -> p b d", b=NB)

    def compute(nc, v, act, loaded, free):
        V = nc.vector
        loaded(0)
        for i in range(1, UG):
            loaded(i)
            v(V.tensor_tensor(A, A, B[i % 2], ALU.add))
            free(i + 2)
        v(V.tensor_scalar(st[0][:], A[:, :, D], 1e-8, None, ALU.max))
        v(V.reciprocal(st[0][:], st[0][:]))
        v(V.tensor_tensor(TMP, A[:, :, 0:D], bc(st[0][:]), ALU.mult))
        v(V.tensor_tensor(TMP, TMP, X, ALU.add))
        v(V.tensor_scalar(dis, A[:, :, D + 1], 0.5, None, ALU.max))
        act(lambda: nc.scalar.activation(dis, dis, ACT.Sqrt))
        v(V.reciprocal(dis, dis))
        v(V.tensor_scalar(st[0][:], A[:, :, D + 1], 0.5, None, ALU.is_gt))
        v(V.tensor_tensor(dis, dis, st[0][:], ALU.mult))
        layernorm(nc, v, act, L, OUT, room(L, 0, D), TMP)
        g = L["gam"][:].rearrange("p (o d) -> p o d", o=1).to_broadcast([P, NB, D])
        b = L["bet"][:].rearrange("p (o d) -> p o d", o=1).to_broadcast([P, NB, D])
        v(V.tensor_tensor(OUT, OUT, g, ALU.mult))
        v(V.tensor_tensor(OUT, OUT, b, ALU.add))
        v(V.tensor_tensor(OUT, OUT, X, ALU.add))
        layernorm(nc, v, act, L, X, TMP, OUT)
    NodePhase(nc, L, "n1", [(A, rows(0))] + [(B[i % 2], rows(i)) for i in range(1, UG)],
              [(node_rows(L["tab_h"][0], 0, D, 0), X)], compute)


def nodes2a(nc, L):
    A, TMP, OUT = room(L, 0, D), L["TMP"], L["OUT"]

    def compute(nc, v, act, k):
        v(nc.vector.tensor_tensor(TMP[:, k, :], A[:, k, :], OUT[:, k, :], ALU.add))
        v(nc.vector.tensor_scalar(TMP[:, k, :], TMP[:, k, :], 0.0, None, ALU.max))
    NodePhase(nc, L, "n2a", in_halves(A, node_rows(L["rank48"][0], 0, D, 0)),
              in_halves(node_rows(L["tab_h"][1], 0, D, 0), TMP), compute, halves=True)


def nodes2b(nc, L):
    A, X, TMP, OUT = room(L, 0, D), L["X"], L["TMP"], L["OUT"]

    def compute(nc, v, act, k):
        V = nc.vector
        x, t = X[:, k, :], TMP[:, k, :]
        v(V.tensor_tensor(t, A[:, k, :], OUT[:, k, :], ALU.add))
        v(V.tensor_tensor(t, t, x, ALU.add))
        layernorm(nc, v, act, L, x, OUT[:, k, :], t, k)
        v(V.tensor_tensor(t, x, bc(L["dis"][:, k]), ALU.mult))
    NodePhase(nc, L, "n2b", in_halves(A, node_rows(L["rank48"][1], 0, D, 0)),
              in_halves(node_rows(L["tab_h"][2], 0, D, 0), TMP), compute, halves=True)


def nodes3a(nc, L):
    H = NB // 2
    A = room(L, 0, 3 * D, H)
    OUT, TMP = L["OUT"], L["TMP"]
    dis, d2 = L["dis"][:], L["stat"][0][:]

    def compute(nc, v, act, loaded, free):
        V = nc.vector
        v(V.tensor_tensor(d2, dis, dis, ALU.mult))
        for h in range(2):
            loaded(h)
            o, t = OUT[:, h * H:(h + 1) * H, :], TMP[:, h * H:(h + 1) * H, :]
            dh = dis[:, h * H:(h + 1) * H].rearrange("p (b o) -> p b o", o=1).to_broadcast([P, H, D])
            d2h = d2[:, h * H:(h + 1) * H].rearrange("p (b o) -> p b o", o=1).to_broadcast([P, H, D])
            v(V.tensor_tensor(t, A[:, :, 2 * D:3 * D], A[:, :, D:2 * D], ALU.subtract))
            v(V.tensor_tensor(t, t, dh, ALU.mult))
            v(V.tensor_tensor(o, o, t, ALU.add))
            v(V.scalar_tensor_tensor(out=t, in0=A[:, :, 0:D], scalar=-1.0, in1=d2h, op0=ALU.mult, op1=ALU.mult))
            free(h + 1)
    r = L["rank144"]
    NodePhase(nc, L, "n3a", [(A, r[0:NP, :].rearrange("(p b) d -> p b d", b=NB)[:, h * H:(h + 1) * H, :]) for h in range(2)],
              [(node_rows(L["tab_h"][3], 0, D, 0), TMP)], compute)


def nodes3b(nc, L):
    A, X, TMP, OUT = room(L, 0, 2 * D), L["X"], L["TMP"], L["OUT"]

    def compute(nc, v, act, k):
        V = nc.vector
        t, dis = TMP[:, k, :], bc(L["dis"][:, k])
        v(V.scalar_tensor_tensor(out=t, in0=A[:, k, D:2 * D], scalar=-2.0, in1=dis, op0=ALU.mult, op1=ALU.mult))
        v(V.tensor_tensor(OUT[:, k, :], OUT[:, k, :], t, ALU.add))
        v(V.scalar_tensor_tensor(out=t, in0=A[:, k, 0:D], scalar=-2.0, in1=dis, op0=ALU.mult, op1=ALU.mult))
        v(V.tensor_tensor(t, t, X[:, k, :], ALU.subtract))
        v(V.tensor_tensor(t, t, dis, ALU.mult))
    NodePhase(nc, L, "n3b", in_halves(A, node_rows(L["rank96"], 0, 2 * D, 0)),
              in_halves(node_rows(L["tab_h"][4], 0, D, 0), TMP), compute, halves=True)


def nodes3c(nc, L, out):
    A, X, TMP, OUT = room(L, 0, D), L["X"], L["TMP"], L["OUT"]

    def compute(nc, v, act, k):
        V = nc.vector
        t, o = TMP[:, k, :], OUT[:, k, :]
        v(V.scalar_tensor_tensor(out=t, in0=A[:, k, :], scalar=-2.0, in1=bc(L["dis"][:, k]), op0=ALU.mult, op1=ALU.mult))
        v(V.tensor_tensor(t, t, o, ALU.add))
        v(V.tensor_tensor(o, t, X[:, k, :], ALU.add))
        layernorm(nc, v, act, L, t, A[:, k, :], o, k)
    real = out[0:LAST_P * NB, :].rearrange("(p b) d -> p b d", b=NB)
    rest = out[LAST_P * NB:N, :].rearrange("(p b) d -> p b d", p=1)
    NodePhase(nc, L, "n3c", in_halves(A, node_rows(L["rank48"][2], 0, D, 0)),
              in_halves(real, TMP[0:LAST_P, :, :]) + [(rest, TMP[LAST_P:LAST_P + 1, 0:LAST_B, :])], compute, halves=True)


def edge_pass(nc, L, a):
    loc, loc_ns, src_f, cut = L["loc"], L["loc_ns"], L["src_f"], L["cut"]
    ident, ones_row = L["ident"], L["ones_row"]
    WD = D + 1 + GE
    M = D + 2
    with ExitStack() as c:
        def sb(nm, shape, dt=F32):
            return c.enter_context(nc.sbuf_tensor(f"e_{nm}", shape, dt))

        def ps(nm, shape):
            if len(shape) == 2:
                return bank(nc, c, f"e_{nm}", *shape)
            return bank(nc, c, f"e_{nm}", shape[0], shape[1] * shape[2]).rearrange("p (g d) -> p g d", g=shape[1])

        def sem(nm):
            return cleared(nc, c, f"e_{nm}")
        sidx = sb("sidx", [P, UI, UG], I32)
        part = sb("part", [P, 2, UG, 3], BF16)
        wrow = sb("wrow", [P, UI, UG, WD])
        attr = sb("attr", [P, UI, UG, R])
        es = sb("es", [P, UI, UG, GE])
        atT = sb("atT", [2 * R, UG // 2 * P])
        hid = sb("hid", [2 * D, UG // 2 * P])
        hotT = sb("hotT", [P, UG, P])
        eq = sb("eq", [P, 2, UG, P])
        lg = sb("lg", [P, UG])
        tg = sb("tg", [P, UG, GE])
        gt = sb("gt", [P, UG, D])
        msg = sb("msg", [P, UG, M])
        sums = sb("sums", [P, UI, UG, M])
        p_at = ps("p_at", [2 * R, UG // 2 * P])
        p_h = ps("p_h", [2 * D, UG // 2 * P])
        p_g = ps("p_g", [P, UG, D])
        p_s = ps("p_s", [P, UG, P])
        p_l = ps("p_l", [P, UG, P])
        p_r = [ps(f"p_r{i}", [P, UG, WD]) for i in range(2)]
        p_m = ps("p_m", [P, UG, M])
        s_init = sem("attr_cleared")
        s_attr = [sem(f"attr_landed{i}") for i in range(UI // 2)]
        s_wrow = [sem(f"windows_landed{i}") for i in range(UI)]
        s_sidx = sem("scatter_staged")
        s_stg = sem("group_staged")
        s_at = sem("attr_turned")
        s_atc = sem("attr_copied")
        s_h = sem("hidden_summed")
        s_hid = sem("hidden_done")
        s_g = sem("gate_summed")
        s_spr = sem("columns_spread")
        s_hot = sem("onehot_built")
        s_eq = sem("sources_compared")
        s_r = sem("rows_picked")
        s_d = sem("dve_steps")
        s_m = sem("sources_merged")
        s_sum = sem("sums_copied")
        s_put = [sem(f"sums_added{i}") for i in range(UG)]
        clear_all(nc)
        block = c.enter_context(nc.Block())
        LF = (E - E // (2 * UG * P) * (2 * UG * P)) // P
        DS = 5 + UG

        @block.sync
        def _(sp):
            full = E // (2 * UG * P)
            at_v = a["edge_attr_40"][0:full * 2 * UG * P, :].rearrange("(g j p) d -> p g j d", j=2 * UG, p=P)
            es_v = L["emb_edge"].rearrange("(g j p) d -> p g j d", j=2 * UG, p=P)
            sp.wait_ge(s_init, 1)

            def step(it, first, last):
                for s in range(UI):
                    if not first and s % 2 == 0:
                        sp.wait_ge(s_d, (it * UI + (s - UI + 2)) * DS)
                    if s % 2 == 0:
                        nc.sync.nop(nofuse=True)
                        pair = it * 2 + s // 2
                        two = attr[:, s:s + 2, :, :].rearrange("p s j d -> p (s j) d")
                        if not last or pair < full:
                            sp.dma_start(two, at_v[:, bass.ds(pair, 1), :, :].rearrange("p g j d -> p (g j) d")
                                         ).then_inc(s_attr[s // 2], 32)
                        else:
                            lo = full * 2 * UG * P
                            sp.dma_start(two[:, 0:LF, :], a["edge_attr_40"][lo:lo + LF * P, :].rearrange("(j p) d -> p j d", p=P)
                                         ).then_inc(s_attr[s // 2], 16)
                            sp.dma_start(two[0:REST, LF, :], a["edge_attr_40"][lo + LF * P:E, :]).then_inc(s_attr[s // 2], 16)
                        sp.dma_start(es[:, s:s + 2, :, :].rearrange("p s j d -> p (s j) d"),
                                     es_v[:, bass.ds(pair, 1), :, :].rearrange("p g j d -> p (g j) d")
                                     ).then_inc(s_attr[s // 2], 16)
                    if not first and s % 2:
                        sp.wait_ge(s_r, it * UI + (s - UI + 1))
                    nc.sync.nop(nofuse=True)
                    _, at = nc.values_load_multi_w_load_instructions(
                        L["win_row"][0:1, bass.ds((it * UI + s) * UG, UG)], engines=[mybir.EngineType.SP],
                        min_val=0, max_val=NP)
                    for j in range(UG):
                        sp.dma_start(wrow[:, s, j, :], L["tab_rank"][bass.ds(at[j], P), :]).then_inc(s_wrow[s], 16)
            run_steps(nc.sync, step)

        @block.gpsimd
        def _(pool):
            def step(it, first, last):
                for s in range(UI):
                    pool.wait_ge(s_sum, it * UI + (s + 1))
                    pool.wait_ge(s_sidx, it * UI + (s + 1))
                    for j in range(UG):
                        if not (first and s == 0):
                            pool.wait_ge(s_put[j], (it * UI + s) * 16)
                        nc.gpsimd.nop(nofuse=True)
                        nc.gpsimd.indirect_dma_start(
                            out=L["scat"][j][:, :], out_offset=bass.IndirectOffsetOnAxis(ap=sidx[:, s, j:j + 1], axis=0),
                            in_=sums[:, s, j, :], in_offset=None, compute_op=ALU.add).then_inc(s_put[j], 16)
            run_steps(nc.gpsimd, step)
            for j in range(UG):
                pool.wait_ge(s_put[j], 16 * GROUPS)

        @block.scalar
        def _(act):
            def stage(it, s):
                b = s % 2
                if not (isinstance(it, int) and it * UI + s < 2):
                    act.wait_ge(s_spr, it * UI + (s - 1))
                at = (it * UI + s) * UG
                nc.scalar.copy(part[:, b, :, :], L["parts"][:, bass.ds(at, UG), :]).then_inc(s_stg, 1)

            def front(it, s):
                g1 = it * UI + (s + 1)
                act.wait_ge(s_at, g1)
                nc.scalar.copy(atT[:], p_at).then_inc(s_atc, 1)
                act.wait_ge(s_h, g1)
                nc.scalar.activation(hid[:], p_h, ACT.Silu, bias=L["b1c"][:]).then_inc(s_hid, 1)

            stage(0, 0)
            stage(0, 1)
            front(0, 0)

            def step(it, first, last):
                for s in range(UI):
                    if not (last and s == UI - 1):
                        front(it, s + 1)
                    if not (last and s >= UI - 2):
                        stage(it, s + 2)
                    if not first:
                        for j in range(UG):
                            act.wait_ge(s_put[j], (it * UI + (s - UI + 1)) * 16)
                    nc.scalar.copy(sidx[:, s, :], L["scat_i"][:, bass.ds((it * UI + s) * UG, UG)]).then_inc(s_sidx, 1)
                    act.wait_ge(s_m, it * UI + (s + 1))
                    nc.scalar.copy(sums[:, s, :, :], p_m[:]).then_inc(s_sum, 1)
            run_steps(nc.scalar, step)

        @block.tensor
        def _(pe):
            def turn(it, s):
                g1, sl, b = it * UI + (s + 1), s % UI, s % 2
                w_it = it if s < UI else it + 1
                start = isinstance(it, int) and it * UI + s == 0
                pe.wait_ge(s_stg, g1)
                if not start:
                    pe.wait_ge(s_hot, it * UI + s)
                    pe.wait_ge(s_eq, it * UI + s)
                nc.tensor.nop(nofuse=True)
                for j in range(UG):
                    nc.tensor.matmul(p_l[:, j, :], part[:, b, j, 0:1].to_broadcast([P, P]), L["id_b"][:], start=True, stop=True)
                    ins = spread_source(nc, L, p_s[:, j, :], part[:, b, j, :])
                ins.then_inc(s_spr, 1)
                pe.wait_ge(s_attr[sl // 2], w_it * 48 + 48)
                if not start:
                    pe.wait_ge(s_atc, it * UI + s)
                nc.tensor.nop(nofuse=True)
                for j in range(UG // 2):
                    ins = nc.tensor.transpose(p_at[:, j * P:(j + 1) * P],
                                              attr[:, sl, 2 * j:2 * j + 2, :].rearrange("p g d -> p (g d)"), ident[:])
                ins.then_inc(s_at, 1)

            def hidden(it, s):
                pe.wait_ge(s_atc, it * UI + (s + 1))
                if not (isinstance(it, int) and it * UI + s == 0):
                    pe.wait_ge(s_hid, it * UI + s)
                nc.tensor.nop(nofuse=True)
                nc.tensor.matmul(p_h, L["w1T"][:], atT[:], start=True, stop=True).then_inc(s_h, 1)

            def pick(it, s):
                sl, b = s % UI, s % 2
                w_it = it if s < UI else it + 1
                pe.wait_ge(s_hot, it * UI + (s + 1))
                pe.wait_ge(s_wrow[sl], w_it * (16 * UG) + 16 * UG)
                if not (isinstance(it, int) and it * UI + s < 2):
                    pe.wait_ge(s_d, (it * UI + (s - 1)) * DS)
                nc.tensor.nop(nofuse=True)
                for j in range(UG):
                    ins = nc.tensor.matmul(p_r[b][:, j, :], hotT[:, j, :], wrow[:, sl, j, :], start=True, stop=True)
                ins.then_inc(s_r, 1)

            def merge(it, s):
                pe.wait_ge(s_d, (it * UI + s) * DS)
                if not (isinstance(it, int) and it * UI + s < 2):
                    pe.wait_ge(s_sum, it * UI + (s - 1))
                nc.tensor.nop(nofuse=True)
                for j in range(UG):
                    ins = nc.tensor.matmul(p_m[:, j, :], eq[:, (s - 1) % 2, j, :], msg[:, j, :], start=True, stop=True)
                ins.then_inc(s_m, 1)

            def gate(it, s):
                pe.wait_ge(s_hid, it * UI + (s + 1))
                nc.tensor.nop(nofuse=True)
                for j in range(UG // 2):
                    two = p_g[:, 2 * j:2 * j + 2, :].rearrange("p g d -> p (g d)")
                    nc.tensor.matmul(two, ones_row[:], L["b2r"][:], start=True, stop=False)
                    ins = nc.tensor.matmul(two, hid[:, j * P:(j + 1) * P], L["w2T"][:], start=False, stop=True)
                ins.then_inc(s_g, 1)

            turn(0, 0)
            hidden(0, 0)
            pick(0, 0)

            def step(it, first, last):
                for s in range(UI):
                    more = not (last and s == UI - 1)
                    if more:
                        turn(it, s + 1)
                    if not (first and s == 0):
                        merge(it, s)
                    gate(it, s)
                    if more:
                        hidden(it, s + 1)
                        pick(it, s + 1)
            run_steps(nc.tensor, step)
            merge(STEPS, 0)

        @block.vector
        def _(dve):
            V = nc.vector
            V.memset(attr[:], 0.0).then_inc(s_init, 1)

            def c4(t):
                return t.rearrange("p (g o) -> p g o", o=1)

            def compare(it, s):
                b = s % 2
                start = isinstance(it, int) and it * UI + s == 0
                dve.wait_ge(s_spr, it * UI + (s + 1))
                if not start:
                    dve.wait_ge(s_r, it * UI + s)
                V.tensor_scalar(hotT[:], p_l[:], L["iota_col"][:], None, ALU.is_equal).then_inc(s_hot, 1)
                if not (isinstance(it, int) and it * UI + s < 2):
                    dve.wait_ge(s_m, it * UI + (s - 1))
                V.tensor_tensor(eq[:, b, :, :], p_s[:], c4(src_f[:, bass.ds((it * UI + s) * UG, UG)]).to_broadcast([P, UG, P]),
                                ALU.is_equal).then_inc(s_eq, 1)

            compare(0, 0)

            def step(it, first, last):
                for s in range(UI):
                    b, n = s % 2, [0]
                    g = it * UI + s
                    if not (last and s == UI - 1):
                        compare(it, s + 1)

                    def v(ins, wait=True):
                        n[0] += 1
                        ins.then_inc(s_d, 1)
                        if wait:
                            dve.wait_ge(s_d, g * DS + n[0])

                    dve.wait_ge(s_attr[s // 2], it * 48 + 48)
                    dve.wait_ge(s_r, it * UI + (s + 1))
                    if not (first and s == 0):
                        dve.wait_ge(s_d, g * DS)
                    v(V.tensor_tensor(tg[:], es[:, s, :, :], p_r[b][:, :, D + 1:WD], ALU.mult), False)
                    v(V.tensor_tensor(gt[:], p_r[b][:, :, 0:D], c4(cut[:, bass.ds(g * UG, UG)]).to_broadcast([P, UG, D]),
                                      ALU.mult), False)
                    if not (first and s == 0):
                        dve.wait_ge(s_m, it * UI + s)
                    v(V.tensor_scalar(msg[:, :, D + 1], loc_ns[:, bass.ds(g * UG, UG)], 0.0, None, ALU.is_ge), False)
                    dve.wait_ge(s_d, g * DS + 1)
                    v(V.tensor_reduce(lg[:], tg[:], AX.X, ALU.add), False)
                    v(V.tensor_copy(msg[:, :, D], p_r[b][:, :, D]), False)
                    dve.wait_ge(s_d, g * DS + 4)
                    dve.wait_ge(s_g, it * UI + (s + 1))
                    for j in range(UG):
                        v(V.scalar_tensor_tensor(out=msg[:, j, 0:D], in0=p_g[:, j, :], scalar=lg[:, j:j + 1],
                                                 in1=gt[:, j, :], op0=ALU.add, op1=ALU.mult), False)
                    assert n[0] == DS
            run_steps(nc.vector, step)


_INS = ['x', 'src', 'dst', 'edge_attr_40', 'edge_weight', 'edge_weight1', 'node_type_119', 'node_vec', 'L1_gnn_W1',
        'L1_gnn_b1', 'L1_gnn_W2', 'L1_gnn_b2', 'L1_gnn_emb', 'L1_gnn_adaptW', 'L1_gnn_gamma', 'L1_gnn_beta',
        'L2_gnn_w_rel1', 'L2_gnn_w_root1', 'L2_gnn_b1', 'L2_gnn_w_rel2', 'L2_gnn_w_root2', 'L2_gnn_b2',
        'L3_gnn_weight', 'L3_gnn_bias']


def kernel(**inputs):
    import numpy as _np
    import concourse.bacc as _bacc
    from concourse import mybir as _mybir
    from concourse.bass_utils import run_bass_kernel_spmd as _run

    nc = _bacc.Bacc("TRN2", target_bir_lowering=False, num_devices=1)
    arrays, args = {}, {}
    for name in _INS:
        v = _np.ascontiguousarray(inputs[name])
        arrays[f"in_{name}_dram"] = v
        args[name] = nc.dram_tensor(f"in_{name}_dram", v.shape, _mybir.dt.from_np(v.dtype), kind="ExternalInput").ap()
    out = nc.dram_tensor("out_0_dram", (N, D), _mybir.dt.float32, kind="ExternalOutput").ap()
    gnn(nc, args, out)
    r = _run(nc, [arrays], core_ids=[0])
    return r.results[0]["out_0_dram"]
```
